# Optimizing a Trainium2 kernel written in Bass

```python
import numpy as np
import jax
import jax.numpy as jnp

def _softmax(x, axis=-1):
    return jax.nn.softmax(x, axis=axis)

def _gelu(x):
    return jax.nn.gelu(x, approximate=True)

def _silu(x):
    return jax.nn.silu(x)

def _sigmoid(x):
    return jax.nn.sigmoid(x)

def _layernorm(x, axis=-1, eps=1e-05):
    m = jnp.mean(x, axis=axis, keepdims=True)
    v = jnp.var(x, axis=axis, keepdims=True)
    return (x - m) / jnp.sqrt(v + eps)

def _scatter_add(tgt, idx, src, axis=0):
    return tgt.at[idx].add(src)

def _segment_sum(src, seg, n):
    return jax.ops.segment_sum(src, seg, n)
kernel_name = 'mk_gnn_ffn_d1_gnn_r8_95716d'

def setup_inputs(seed: int=0):
    np.random.seed(seed)
    _w = jnp.asarray

    def _rec_inputs():
        import jax
        import jax.numpy as jnp
        _gk = jax.random.key(seed)
        x = -0.0005963 + 1.001 * jax.random.normal(jax.random.fold_in(_gk, 1), (384, 1024), jnp.float32)
        _s = jax.random.randint(jax.random.fold_in(_gk, 2), (6144,), 0, 384, jnp.int32)
        _d = jax.random.randint(jax.random.fold_in(_gk, 3), (6144,), 0, 384, jnp.int32)
        _loop = jnp.arange(384, dtype=jnp.int32)
        src = jnp.concatenate([_s, _d, _loop])
        dst = jnp.concatenate([_d, _s, _loop])
        _o = jnp.argsort(dst, stable=True)
        src = src[_o]
        dst = dst[_o]
        edge_type_5 = jax.random.randint(jax.random.fold_in(_gk, 12), (12672,), 0, 5, jnp.int32)
        return (x, src, dst, edge_type_5)
    x, src, dst, edge_type_5 = _rec_inputs()

    def _L0_gnn_setup():
        import jax, jax.numpy as jnp
        import numpy as np
        N = 384
        E = 12288
        IN_F = 1024
        OUT_F = 1024
        H = 16
        D = OUT_F // H
        NUM_ETYPES = 4

        def _build_mask(edge_index, edge_type, edge_type_weights, dtype):
            src, dst = (edge_index[0], edge_index[1])
            w = jax.nn.softplus(edge_type_weights)
            mask = jnp.full((N, N), -jnp.inf, dtype=dtype)
            mask = mask.at[src, dst].set(w[edge_type - 1])
            diag = jnp.diagonal(mask)
            idx = jnp.arange(N)
            mask = mask.at[idx, idx].set(jnp.where(jnp.isneginf(diag), w[3], diag))
            return mask
        key = jax.random.key(seed)
        ks = jax.random.split(key, 20)
        p = lambda k, shape: jax.random.normal(k, shape, dtype=jnp.float32) * 0.02
        return {'x': jax.random.normal(ks[0], (N, IN_F), dtype=jnp.float32), 'edge_index': jax.random.randint(ks[1], (2, E), 0, N), 'edge_type': jax.random.randint(ks[2], (E,), 1, NUM_ETYPES + 1), 'edge_type_weights': jnp.ones((NUM_ETYPES,), jnp.float32) + 0.1 * jax.random.normal(ks[3], (NUM_ETYPES,), dtype=jnp.float32), 'wq': p(ks[4], (OUT_F, IN_F)), 'bq': p(ks[5], (OUT_F,)), 'wk': p(ks[6], (OUT_F, IN_F)), 'bk': p(ks[7], (OUT_F,)), 'wv': p(ks[8], (OUT_F, IN_F)), 'bv': p(ks[9], (OUT_F,)), 'wiq': p(ks[10], (OUT_F, OUT_F)), 'biq': p(ks[11], (OUT_F,)), 'wik': p(ks[12], (OUT_F, OUT_F)), 'bik': p(ks[13], (OUT_F,)), 'wiv': p(ks[14], (OUT_F, OUT_F)), 'biv': p(ks[15], (OUT_F,)), 'wo': p(ks[16], (OUT_F, OUT_F)), 'bo': p(ks[17], (OUT_F,))}
    _L0_gnn_all = _L0_gnn_setup()
    _L0_gnn_in = {k: v for k, v in _L0_gnn_all.items() if k in ('edge_type_weights', 'wq', 'bq', 'wk', 'bk', 'wv', 'bv', 'wiq', 'biq', 'wik', 'bik', 'wiv', 'biv', 'wo', 'bo')}
    del _L0_gnn_all

    def _L0_ffn_setup():
        import jax, jax.numpy as jnp
        import numpy as np
        EPS = 1e-05

        def _quantize(W):
            gamma = jnp.mean(jnp.abs(W))
            return jnp.clip(jnp.round(W / (gamma + EPS)), -1.0, 1.0)
        key = jax.random.key(seed)
        k_x, k_w1, k_b1, k_w2, k_b2 = jax.random.split(key, 5)
        n_embd = 1024
        d_ff = 4 * n_embd
        B, S = (4, 512)
        bound1 = 1.0 / np.sqrt(n_embd)
        bound2 = 1.0 / np.sqrt(d_ff)
        x = jax.random.normal(k_x, (B, S, n_embd), dtype=jnp.float32)
        W1 = jax.random.uniform(k_w1, (d_ff, n_embd), jnp.float32, -bound1, bound1)
        b1 = jax.random.uniform(k_b1, (d_ff,), jnp.float32, -bound1, bound1)
        W2 = jax.random.uniform(k_w2, (n_embd, d_ff), jnp.float32, -bound2, bound2)
        b2 = jax.random.uniform(k_b2, (n_embd,), jnp.float32, -bound2, bound2)
        return {'x': x, 'W1': W1, 'b1': b1, 'W2': W2, 'b2': b2}
    _L0_ffn_all = _L0_ffn_setup()
    _L0_ffn_in = {k: v for k, v in _L0_ffn_all.items() if k in ('W1', 'b1', 'W2', 'b2')}
    del _L0_ffn_all
    return {'x': x, 'src': src, 'dst': dst, 'edge_type_5': edge_type_5, 'L0_gnn_edge_type_weights': _L0_gnn_in['edge_type_weights'], 'L0_gnn_wq': _L0_gnn_in['wq'], 'L0_gnn_bq': _L0_gnn_in['bq'], 'L0_gnn_wk': _L0_gnn_in['wk'], 'L0_gnn_bk': _L0_gnn_in['bk'], 'L0_gnn_wv': _L0_gnn_in['wv'], 'L0_gnn_bv': _L0_gnn_in['bv'], 'L0_gnn_wiq': _L0_gnn_in['wiq'], 'L0_gnn_biq': _L0_gnn_in['biq'], 'L0_gnn_wik': _L0_gnn_in['wik'], 'L0_gnn_bik': _L0_gnn_in['bik'], 'L0_gnn_wiv': _L0_gnn_in['wiv'], 'L0_gnn_biv': _L0_gnn_in['biv'], 'L0_gnn_wo': _L0_gnn_in['wo'], 'L0_gnn_bo': _L0_gnn_in['bo'], 'L0_ffn_W1': _L0_ffn_in['W1'], 'L0_ffn_b1': _L0_ffn_in['b1'], 'L0_ffn_W2': _L0_ffn_in['W2'], 'L0_ffn_b2': _L0_ffn_in['b2']}

def reference(x, src, dst, edge_type_5, L0_gnn_edge_type_weights, L0_gnn_wq, L0_gnn_bq, L0_gnn_wk, L0_gnn_bk, L0_gnn_wv, L0_gnn_bv, L0_gnn_wiq, L0_gnn_biq, L0_gnn_wik, L0_gnn_bik, L0_gnn_wiv, L0_gnn_biv, L0_gnn_wo, L0_gnn_bo, L0_ffn_W1, L0_ffn_b1, L0_ffn_W2, L0_ffn_b2):
    import jax
    import jax.numpy as jnp

    def _L0_gnn_ref(x, edge_index, edge_type, edge_type_weights, wq, bq, wk, bk, wv, bv, wiq, biq, wik, bik, wiv, biv, wo, bo):
        import jax, jax.numpy as jnp
        import numpy as np
        N = 384
        E = 12288
        IN_F = 1024
        OUT_F = 1024
        H = 16
        D = OUT_F // H
        NUM_ETYPES = 4

        def _build_mask(edge_index, edge_type, edge_type_weights, dtype):
            src, dst = (edge_index[0], edge_index[1])
            w = jax.nn.softplus(edge_type_weights)
            mask = jnp.full((N, N), -jnp.inf, dtype=dtype)
            mask = mask.at[src, dst].set(w[edge_type - 1])
            diag = jnp.diagonal(mask)
            idx = jnp.arange(N)
            mask = mask.at[idx, idx].set(jnp.where(jnp.isneginf(diag), w[3], diag))
            return mask
        q = x @ wq.T + bq
        k = x @ wk.T + bk
        v = x @ wv.T + bv
        q2 = (q @ wiq.T + biq).reshape(N, H, D).transpose(1, 0, 2)
        k2 = (k @ wik.T + bik).reshape(N, H, D).transpose(1, 0, 2)
        v2 = (v @ wiv.T + biv).reshape(N, H, D).transpose(1, 0, 2)
        mask = _build_mask(edge_index, edge_type, edge_type_weights, x.dtype)
        scale = 1.0 / np.sqrt(D).astype(np.float32)
        scores = jnp.einsum('hnd,hmd->hnm', q2, k2) * scale + mask[None]
        attn = jax.nn.softmax(scores, axis=-1)
        out = jnp.einsum('hnm,hmd->hnd', attn, v2)
        out = out.transpose(1, 0, 2).reshape(N, OUT_F)
        return out @ wo.T + bo

    def _L0_ffn_ref(x, W1, b1, W2, b2):
        import jax, jax.numpy as jnp
        import numpy as np
        EPS = 1e-05

        def _quantize(W):
            gamma = jnp.mean(jnp.abs(W))
            return jnp.clip(jnp.round(W / (gamma + EPS)), -1.0, 1.0)
        Wq1 = _quantize(W1)
        Wq2 = _quantize(W2)
        h = jax.nn.relu(jnp.einsum('bsd,fd->bsf', x, Wq1) + b1)
        out = jnp.einsum('bsf,df->bsd', h, Wq2) + b2
        return out
    edge_index = jnp.stack([src, dst])
    x = x + _L0_gnn_ref(_layernorm(x, axis=-1), edge_index, edge_type_5, L0_gnn_edge_type_weights, L0_gnn_wq, L0_gnn_bq, L0_gnn_wk, L0_gnn_bk, L0_gnn_wv, L0_gnn_bv, L0_gnn_wiq, L0_gnn_biq, L0_gnn_wik, L0_gnn_bik, L0_gnn_wiv, L0_gnn_biv, L0_gnn_wo, L0_gnn_bo)
    x = x + _L0_ffn_ref(_layernorm(x, axis=-1)[None], L0_ffn_W1, L0_ffn_b1, L0_ffn_W2, L0_ffn_b2)[0]
    return x

_drawn_inputs = setup_inputs


def setup_inputs(seed=0):
    import zlib

    import numpy as np

    out = dict(_drawn_inputs(seed))
    spreads = {}
    factors = {'L0_gnn_edge_type_weights': 61.296,
     'L0_gnn_wq': 8.0,
     'L0_gnn_bq': 8.0,
     'L0_gnn_wk': 8.0,
     'L0_gnn_bk': 64.0,
     'L0_gnn_bv': 8.0,
     'L0_gnn_wiq': 8.0,
     'L0_gnn_biq': 24.002,
     'L0_gnn_wik': 8.0,
     'L0_gnn_bik': 64.0,
     'L0_gnn_biv': 5.394,
     'L0_gnn_bo': 3.43,
     'L0_ffn_b1': 64.0,
     'L0_ffn_b2': 64.0}
    for name, (base, spread) in spreads.items():
        noise = np.random.default_rng([zlib.crc32(name.encode()), seed]).standard_normal(out[name].shape)
        drawn = base * np.exp(spread * noise) if base else spread * noise
        out[name] = jnp.asarray(drawn.astype(out[name].dtype))
    for name, factor in factors.items():
        out[name] = (out[name] * factor).astype(out[name].dtype)
    return out
```

```python
from contextlib import ExitStack

import concourse.bass as bass
from concourse import mybir

F32 = mybir.dt.float32
F32R = mybir.dt.float32r
BF16 = mybir.dt.bfloat16
F16 = mybir.dt.float16
I32 = mybir.dt.int32
ALU = mybir.AluOpType
ACT = mybir.ActivationFunctionType
AX = mybir.AxisListType

P = 128
N = 384
NT = N // P
D = 1024
KO = D // P
HD = 64
PAIRS = D // (2 * HD)
F = 4 * D
FT = F // P
E = 12672
CH = E // P
CPI = 12
CPS = CPI // 3
CH0 = CH - KO * CPI
GROUP_A = CH0 + 4 * CPI
ETYPES = 4
EPS = 1e-5
NEG = -3.0e38
EXP_BASE = 20
SLABS = 56
H_SCALE = 1024.0
H_SUM_MAX = 1024.0

BANK_PROJ, BANK_SCORE, BANK_TURN, BANK_PV = 0, 3, 5, 7
BANK_MASK = 3
BANK_HID, BANK_Y = 0, 2


def wait(eng, sem, value):
    if not (isinstance(value, int) and value <= 0):
        eng.wait_ge(sem, value)


def gnn_ffn_kernel(nc, x, src_rows, dst_rows, src_cols, dst_cols, type_cols, edge_w, w_slabs, biases,
                   ffn_slabs, b1, b2, out):
    ctx = ExitStack()
    early, edges, pairs = ExitStack(), ExitStack(), ExitStack()
    late = ExitStack()
    with ctx:
        def sb(name, shape, dt, scope=ctx):
            return scope.enter_context(nc.sbuf_tensor(name, shape, dt))

        def sem(name):
            return ctx.enter_context(nc.semaphore(name))

        xs = sb("xs", [P, NT, D], F32)
        raw = sb("raw", [P, 3, D], F32)
        w_hi = sb("w_hi", [P, 3, D], F32R)
        w_lo = sb("w_lo", [P, 3, D], F32R)
        hT_hi = sb("hT_hi", [P, KO, N], F32R)
        hT_lo = sb("hT_lo", [P, KO, N], F32R)
        stream = sb("stream", [P, 4, D], F32)
        bias = sb("bias", [P, 7, KO], F32)
        b1c = sb("b1c", [P, FT], F32)
        b1s = sb("b1s", [P, FT], F32)
        b2r = sb("b2r", [P, D], F32)
        ident = sb("ident", [P, P], F32)
        ones = sb("ones", [P, P], F32)
        stats = sb("stats", [P, NT, 2, 6], F32)
        mv = sb("mv", [P, NT, 2], F32)
        ln_s = sb("ln_s", [P, 6, NT], F32)
        gacc = sb("gacc", [P, 2 * FT // 2], F32)
        gsum = sb("gsum", [P, 2], F32)
        thr = sb("thr", [P, 4], F32)
        hs = sb("hs", [P, 8], F32)
        hsi = sb("hsi", [P, 4], I32)
        qkv_hi = [sb(f"qkv_hi{j}", [P, KO, N], F32R, early) for j in range(3)]
        qkv_lo = [sb(f"qkv_lo{j}", [P, KO, N], F32R, early) for j in range(3)]
        mask8 = sb("mask8", [P, NT, N], F32, early)
        probs = sb("probs", [P, 6, N], F32, early)
        sm = sb("sm", [P, 4, 6], F32, early)
        expo = sb("expo", [P, NT, N], I32, early)
        ew = sb("ew", [P, ETYPES], F32, early)
        ew_s = sb("ew_s", [P, 5, ETYPES], F32, early)
        src_hot = sb("src_hot", [P, 4, N], BF16, edges)
        dst_hot = sb("dst_hot", [P, 4, N], BF16, edges)
        nodes = sb("nodes", [P, N], F16, edges)
        later = sb("later", [P, P], F32, edges)
        ident_b = sb("ident_b", [P, P], BF16, edges)
        diag_hot = sb("diag_hot", [P, NT, N], BF16, edges)
        zeros_b = sb("zeros_b", [P, N], BF16, edges)
        tile_row = sb("tile_row", [P, NT], F32, edges)
        rows_i = sb("rows_i", [CH, 2, P], I32, edges)
        key_rows = sb("key_rows", [CH, P], F32, edges)
        cols_i = sb("cols_i", [P, 3, CH], I32, edges)
        cols_f = sb("cols_f", [P, 2, CH], F32, edges)
        key_col = sb("key_col", [P, CH], F32, edges)
        ebase = sb("ebase", [P, CH], I32, edges)
        etmp = sb("etmp", [P, 2, CH], I32, edges)
        later_n = sb("later_n", [P, CPI], F32, edges)
        value = sb("value", [P, CPI], F32, edges)
        edges.close()
        q2_hi = sb("q2_hi", [P, N], F32R, pairs)
        q2_lo = sb("q2_lo", [P, N], F32R, pairs)
        k2_hi = sb("k2_hi", [P, N], F32R, pairs)
        k2_lo = sb("k2_lo", [P, N], F32R, pairs)
        v2T = sb("v2T", [P, N], F32, pairs)
        v2_hi = sb("v2_hi", [P, NT, P], F32R, pairs)
        v2_lo = sb("v2_lo", [P, NT, P], F32R, pairs)
        pT_hi = sb("pT_hi", [P, NT, N], F32R, pairs)
        pT_lo = sb("pT_lo", [P, NT, N], F32R, pairs)
        pairs.close()
        early.close()
        turned = sb("turned", [P, N], F32, late)
        h2_hi = sb("h2_hi", [P, KO, N], F16, late)
        h2_lo = sb("h2_lo", [P, KO, N], F16, late)
        minus = sb("minus", [P, 2, 2, D], F16, late)
        tern = sb("tern", [P, 2, 2, D], F16, late)
        act = sb("act", [P, 2, N], F32, late)
        act_hi = sb("act_hi", [P, 2, N], F16, late)
        act_lo = sb("act_lo", [P, 2, N], F16, late)
        late.close()
        bank = [ctx.enter_context(nc.psum_tensor(f"bank{i}", [P, 512], F32)) for i in range(8)]
        key_dram = nc.dram_tensor("key_scratch", [CH * P], F32, kind="Internal").ap()
        m_i = probs[:, 0:2].bitcast(I32)
        m_f = probs[:, 2]
        key_bc = probs[:, 0:4, :]

        x_in = [sem(f"x_in{n}") for n in range(NT)]
        edges_in, const_in, rows_in = sem("edges_in"), sem("const_in"), sem("rows_in")
        raw_in = [sem(f"raw_in{j}") for j in range(3)]
        key_out, key_in = sem("key_out"), sem("key_in")
        gamma_in = [sem(f"gamma_in{u}") for u in range(2)]
        consts = sem("consts")
        key_made = sem("key_made")
        pre = sem("pre")
        a_pre = sem("a_pre")
        w_hi_made, w_lo_made, slab_done = sem("w_hi_made"), sem("w_lo_made"), sem("slab_done")
        proj_hi_made, proj_lo_made = sem("proj_hi_made"), sem("proj_lo_made")
        ln_turned, ln_hi, ln_lo = sem("ln_turned"), sem("ln_hi"), sem("ln_lo")
        var_made, sd_made = sem("var_made"), sem("sd_made")
        h_made = sem("h_made")
        gamma_done = sem("gamma_done")
        keys_used, counted, valued = sem("keys_used"), sem("counted"), sem("valued")
        hot_made, hot_used = sem("hot_made"), sem("hot_used")
        group_done, group_read = sem("group_done"), sem("group_read")
        ew_exp, ew_done, mask_made = sem("ew_exp"), sem("ew_done"), sem("mask_made")
        scored, score_max, max_neg, exped, inv_made, normed = (
            sem("scored"), sem("score_max"), sem("max_neg"), sem("exped"), sem("inv_made"), sem("normed"))
        turned_done, turn_hi, turn_lo = sem("turned_done"), sem("turn_hi"), sem("turn_lo")
        pv_done, pv_hi, pv_lo = sem("pv_done"), sem("pv_hi"), sem("pv_lo")
        gsum_made, gsum_all = sem("gsum_made"), sem("gsum_all")
        o_biased, o_turned, x_added = sem("o_biased"), sem("o_turned"), sem("x_added")
        b1_max, b1_all = sem("b1_max"), sem("b1_all")
        ffn_in = [[sem(f"ffn_in{m}{u}") for u in range(2)] for m in range(2)]
        minus_made, tern_made = sem("minus_made"), sem("tern_made")
        hid_done, relu_done, act_hi_made, act_lo_made = sem("hid_done"), sem("relu_done"), sem("act_hi_made"), sem("act_lo_made")
        y_step, y_done, y_ready, out_done = sem("y_step"), sem("y_done"), sem("y_ready"), sem("out_done")
        b2_added = sem("b2_added")
        scores_seen, slabs_seen = sem("scores_seen"), sem("slabs_seen")

        block = ctx.enter_context(nc.Block())
        stage3 = 2 * PAIRS * 3
        LN_UNITS = KO

        @block.sync
        def _(sp):
            sp.dma_start(rows_i[:, 0], src_rows).then_inc(rows_in, 16)
            sp.dma_start(rows_i[:, 1], dst_rows).then_inc(rows_in, 16)
            for n in range(NT):
                sp.dma_start(xs[:, n], x[n * P:(n + 1) * P]).then_inc(x_in[n], 16)
            for a, cols in enumerate((src_cols, dst_cols, type_cols)):
                sp.dma_start(cols_i[:, a], cols).then_inc(edges_in, 16)
            sp.dma_start(ew[:], edge_w.partition_broadcast(P)).then_inc(edges_in, 16)
            for j in range(3):
                sp.dma_start(raw[:, j], w_slabs[j]).then_inc(raw_in[j], 16)
            sp.dma_start(bias[:], biases).then_inc(const_in, 16)
            sp.dma_start(b1c[:], b1).then_inc(const_in, 16)
            sp.dma_start(b2r[:], b2.partition_broadcast(P)).then_inc(const_in, 16)
            sp.wait_ge(key_made, 1)
            sp.dma_start(key_dram.rearrange("(c p) -> c p", p=P), key_rows[:]).then_inc(key_out, 16)
            sp.wait_ge(key_out, 16)
            sp.dma_start(key_bc[:, 0, :], key_dram[0:CH0 * P].partition_broadcast(P)).then_inc(key_in, 16)

            def fetch_keys(i):
                sp.wait_ge(keys_used, i + 1)
                sp.dma_start(key_bc.rearrange("p a b -> p (a b)"),
                             key_dram[bass.ds(CH0 * P + i * (CPI * P), CPI * P)].partition_broadcast(P)
                             ).then_inc(key_in, 16)

            def fetch_slab(s, j):
                wait(sp, w_lo_made, s - 2)
                sp.dma_start(raw[:, j], w_slabs[s]).then_inc(raw_in[j], 16)

            def fetch_gamma(g, u):
                if isinstance(g, int) and g < 2:
                    sp.wait_ge(ln_turned, LN_UNITS)
                else:
                    sp.wait_ge(gamma_done, g - 1)
                sp.dma_start(stream[:, 2 * u:2 * u + 2],
                             ffn_slabs[bass.ds(g * 2, 2)].rearrange("t p c -> p t c")).then_inc(gamma_in[u], 16)

            def iteration(i, stage):
                fetch_gamma(i * 2, 0)
                fetch_slab(i * 3 + 3, 0)
                fetch_slab(i * 3 + 4, 1)
                fetch_gamma(i * 2 + 1, 1)
                fetch_slab(i * 3 + 5, 2)

            fetch_keys(0)
            iteration(0, 1)
            with sp.Fori(1, KO) as i:
                fetch_keys(i)
                iteration(i, 1)
            with sp.Fori(KO, KO + PAIRS) as i:
                iteration(i, 2)
            fetch_slab(stage3 + 3, 0)
            fetch_slab(stage3 + 4, 1)
            fetch_slab(stage3 + 5, 2)
            fetch_slab(stage3 + 6, 0)
            fetch_slab(stage3 + 7, 1)

            def fetch_ffn(t, u):
                for m in range(2):
                    if isinstance(t, int) and t < 2:
                        sp.wait_ge(gamma_done, FT)
                    else:
                        sp.wait_ge(tern_made, t * 2 + m - 3)
                    sp.dma_start(stream[:, 2 * m + u], ffn_slabs[t + m * FT]).then_inc(ffn_in[m][u], 16)

            for u in range(2):
                fetch_ffn(u, u)
            with sp.Fori(1, FT // 2) as i:
                for u in range(2):
                    fetch_ffn(i * 2 + u, u)
            for n in range(NT):
                sp.wait_ge(y_ready, 2 * n + 2)
                sp.dma_start(out[n * P:(n + 1) * P], xs[:, n]).then_inc(out_done, 16)
            sp.wait_ge(out_done, 16 * NT)

        @block.gpsimd
        def _(pool):
            g = nc.gpsimd
            g.memset(ones[:], 1.0).then_inc(consts, 1)
            g.memset(zeros_b[:], 0.0).then_inc(consts, 1)
            pool.wait_ge(consts, 2)
            g.affine_select(out=ident[:], in_=ones[:], compare_op=ALU.is_equal, fill=0.0, base=0,
                            pattern=[[1, P]], channel_multiplier=-1).then_inc(consts, 1)
            g.affine_select(out=later[:], in_=ones[:], compare_op=ALU.is_gt, fill=0.0, base=0,
                            pattern=[[1, P]], channel_multiplier=-1).then_inc(consts, 1)
            g.iota(nodes[:], [[1, N]], base=0, channel_multiplier=0,
                   allow_small_or_imprecise_dtypes=True).then_inc(consts, 1)
            g.iota(tile_row[:], [[P, NT]], base=0, channel_multiplier=1,
                   allow_small_or_imprecise_dtypes=True).then_inc(consts, 1)
            g.iota(ebase[:, 0:GROUP_A], [[ETYPES, GROUP_A]], base=EXP_BASE, channel_multiplier=0).then_inc(consts, 1)
            g.iota(ebase[:, GROUP_A:CH], [[ETYPES, CH - GROUP_A]], base=EXP_BASE,
                   channel_multiplier=0).then_inc(consts, 1)
            pool.wait_ge(consts, 8)
            g.tensor_copy(ident_b[:], ident[:]).then_inc(consts, 1)
            pool.wait_ge(b1_max, 1)
            g.partition_all_reduce(hs[:, 1:2], hs[:, 0:1], P, bass.bass_isa.ReduceOp.max).then_inc(b1_all, 1)

            pool.wait_ge(h_made, 2 * NT)
            for n in range(NT):
                g.tensor_tensor(xs[:, n], xs[:, n], b2r[:], ALU.add).then_inc(b2_added, 1)

            def below(t, u):
                for m in range(2):
                    pool.wait_ge(ffn_in[m][u], (t // 2 + 1) * 16 if isinstance(t, int) else t * 8 + 16 - 8 * u)
                    wait(pool, tern_made, t * 2 + m - 3)
                    pool.sem_inc(slabs_seen, 1)
                    pool.wait_ge(gsum_all, 2)
                    g.tensor_scalar(minus[:, m, u], stream[:, 2 * m + u], thr[:, 2 + m:3 + m], None,
                                    ALU.is_lt).then_inc(minus_made, 1)

            below(0, 0)
            below(1, 1)
            with pool.Fori(1, FT // 2) as i:
                for u in range(2):
                    below(i * 2 + u, u)

        @block.scalar
        def _(eng):
            a = nc.scalar
            count = [0]

            def step(ins):
                count[0] += 1
                ins.then_inc(a_pre, 1)
                eng.wait_ge(a_pre, count[0])

            eng.wait_ge(edges_in, 64)
            step(a.activation(ew_s[:, 0], ew[:], ACT.Abs))
            step(a.activation(ew_s[:, 1], ew_s[:, 0], ACT.Exp, scale=-1.0))
            a.activation(ew_s[:, 2], ew_s[:, 1], ACT.Ln, bias=1.0).then_inc(ew_exp, 1)

            def root(k):
                eng.wait_ge(var_made, k + 1)
                a.activation(ln_s[:, 1], ln_s[:, 0], ACT.Sqrt).then_inc(sd_made, 1)

            root(0)

            def split_w(s, j):
                eng.wait_ge(raw_in[j], (s // 3 + 1) * 16 if isinstance(s, int) else (s - j) // 3 * 16 + 16)
                wait(eng, slab_done, s - 2)
                a.activation(w_hi[:, j], raw[:, j], ACT.Copy).then_inc(w_hi_made, 1)

            def split_at(i, j):
                eng.wait_ge(raw_in[j], i * 16 + 16)
                wait(eng, slab_done, i * 3 + j - 2)
                a.activation(w_hi[:, j], raw[:, j], ACT.Copy).then_inc(w_hi_made, 1)

            split_at(0, 0)
            for ko in range(KO):
                eng.wait_ge(ln_turned, ko + 1)
                a.activation(hT_hi[:, ko], bank[ko][:, 0:N], ACT.Copy).then_inc(ln_hi, 1)

            def magnitudes(g, u):
                eng.wait_ge(gamma_in[u], (g // 2 + 1) * 16 if isinstance(g, int) else g * 8 + 16 - 8 * u)
                flat = stream[:, 2 * u:2 * u + 2].rearrange("p a b -> p (a b)")
                a.activation(flat, flat, ACT.Abs,
                             accum_out=gacc[:, bass.ds(g, 1)]).then_inc(gamma_done, 1)

            eng.wait_ge(const_in, 48)

            def stage1(i):
                for j in range(3):
                    split_at(i + (j + 1) // 3, (j + 1) % 3)
                    if j < 2:
                        magnitudes(i * 2 + j, j)
                    eng.wait_ge(slab_done, i * 3 + j + 1)
                    a.activation(qkv_hi[j][:, bass.ds(i, 1), :], bank[BANK_PROJ + j][:, 0:N], ACT.Identity,
                                 bias=bias[:, j, bass.ds(i, 1)]).then_inc(proj_hi_made, 1)

            stage1(0)
            with eng.Fori(1, KO) as i:
                stage1(i)

            def stage2(i, project, attend):
                p = i - 1
                s = (i + KO) * 3

                def exp(k):
                    eng.wait_ge(max_neg, p * 6 + k + 1)
                    a.activation(probs[:, k], probs[:, k], ACT.Exp, bias=sm[:, 1, k:k + 1], scale=0.125,
                                 accum_out=sm[:, 2, k:k + 1]).then_inc(exped, 1)

                def turn(k):
                    eng.wait_ge(turned_done, p * 7 + k + 2)
                    if k == 3:
                        eng.wait_ge(pv_done, p * 2 + 1)
                    a.activation(pT_hi[:, :, (k % NT) * P:(k % NT + 1) * P],
                                 bank[BANK_TURN + (k + 1) % 2][:, 0:N].rearrange("p (a b) -> p a b", a=NT),
                                 ACT.Copy).then_inc(turn_hi, 1)

                def pv_out(h):
                    rows = slice(HD * h, HD * h + HD)
                    eng.wait_ge(pv_done, p * 2 + h + 1)
                    a.activation(hT_hi[rows, bass.ds(p, 1), :], bank[BANK_PV][rows, 0:N],
                                 ACT.Copy).then_inc(pv_hi, 1)

                def project_out(j):
                    eng.wait_ge(slab_done, s + j + 1)
                    if j < 2:
                        wait(eng, scored, p * 6 + 6)
                        a.activation((q2_hi, k2_hi)[j][:], bank[BANK_PROJ + j][:, 0:N], ACT.Identity,
                                     bias=bias[:, 3 + j, bass.ds(i, 1)]).then_inc(proj_hi_made, 1)
                    else:
                        a.activation(v2T[:], bank[BANK_PROJ + j][:, 0:N], ACT.Identity,
                                     bias=bias[:, 3 + j, bass.ds(i, 1)]).then_inc(proj_hi_made, 1)

                if attend:
                    eng.wait_ge(turned_done, p * 7 + 1)
                    a.activation(v2_hi[:].rearrange("p a b -> p (a b)"), bank[BANK_TURN][:, 0:N],
                                 ACT.Copy).then_inc(turn_hi, 1)
                    exp(0)
                    exp(1)
                if project:
                    split_at(i + KO, 1)
                if attend:
                    exp(2)
                    exp(3)
                if project:
                    magnitudes((i + KO) * 2, 0)
                if attend:
                    turn(0)
                    exp(4)
                    turn(1)
                if project:
                    project_out(0)
                if attend:
                    exp(5)
                    turn(2)
                if project:
                    split_at(i + KO, 2)
                    magnitudes((i + KO) * 2 + 1, 1)
                if attend:
                    pv_out(0)
                    turn(3)
                if project:
                    project_out(1)
                if attend:
                    turn(4)
                    turn(5)
                if project:
                    split_at(i + KO + 1, 0)
                    project_out(2)
                if attend:
                    pv_out(1)

            stage2(0, True, False)
            with eng.Fori(1, PAIRS) as i:
                stage2(i, True, True)
            stage2(PAIRS, False, True)

            def stage3_step(s, j):
                if s + 1 < SLABS:
                    split_at((s + 1) // 3, (s + 1) % 3)
                m = s - stage3
                eng.wait_ge(slab_done, s + 1)
                wait(eng, o_turned, m)
                a.activation(turned[:], bank[BANK_PROJ + j][:, 0:N], ACT.Identity,
                             bias=bias[:, 6, m:m + 1]).then_inc(o_biased, 1)

            for s in range(stage3, SLABS):
                stage3_step(s, s % 3)

            root(1)
            for ko in range(KO):
                eng.wait_ge(ln_turned, KO + ko + 1)
                a.activation(h2_hi[:, ko], bank[ko][:, 0:N], ACT.Copy, scale=H_SCALE).then_inc(ln_hi, 1)

            def relu(t, u):
                eng.wait_ge(hid_done, t + 1)
                wait(eng, act_lo_made, t - 1)
                a.activation(act[:, u], bank[BANK_HID + u][:, 0:N], ACT.Relu, bias=b1s[:, bass.ds(t, 1)],
                             scale=hs[:, 4:5]).then_inc(relu_done, 1)
                eng.wait_ge(relu_done, t + 1)
                wait(eng, y_step, t - 1)
                a.activation(act_hi[:, u], act[:, u], ACT.Copy).then_inc(act_hi_made, 1)

            relu(0, 0)
            relu(1, 1)
            with eng.Fori(1, FT // 2) as i:
                for u in range(2):
                    relu(i * 2 + u, u)

        @block.vector
        def _(dve):
            v = nc.vector
            count = [0]

            def step(ins):
                count[0] += 1
                ins.then_inc(pre, 1)
                dve.wait_ge(pre, count[0])

            dve.sem_inc(pv_lo, 1)
            dve.wait_ge(rows_in, 32)
            v.scalar_tensor_tensor(out=key_rows[:], in0=rows_i[:, 0], scalar=float(N), in1=rows_i[:, 1],
                                   op0=ALU.mult, op1=ALU.add).then_inc(key_made, 1)
            dve.wait_ge(consts, 9)
            dve.wait_ge(edges_in, 64)
            v.tensor_copy(cols_f[:], cols_i[:, 0:2])
            step(v.scalar_tensor_tensor(out=key_col[:], in0=cols_i[:, 0], scalar=float(N), in1=cols_i[:, 1],
                                        op0=ALU.mult, op1=ALU.add))
            step(v.tensor_scalar(etmp[:, 0], cols_i[:, 2], float(ETYPES - 1), None, ALU.add))
            step(v.tensor_scalar(etmp[:, 1], etmp[:, 0], ETYPES - 1, None, ALU.bitwise_and))
            step(v.tensor_tensor(etmp[:, 0], etmp[:, 1], ebase[:], ALU.add))
            step(v.tensor_scalar(etmp[:, 1], etmp[:, 0], 23, None, ALU.logical_shift_left))
            evalue = etmp[:, 1].bitcast(F32)

            def layer_norm(k, h):
                for n in range(NT):
                    if k == 0:
                        dve.wait_ge(x_in[n], 16)
                    for c in range(2):
                        step(v.bn_stats(stats[:, n, c], xs[:, n, c * 512:(c + 1) * 512]))
                    step(v.bn_aggr(mv[:, n], stats[:, n]))
                v.tensor_scalar(ln_s[:, 0], mv[:, :, 1], EPS, None, ALU.add).then_inc(var_made, 1)
                dve.wait_ge(sd_made, k + 1)
                step(v.reciprocal(ln_s[:, 2], ln_s[:, 1]))
                step(v.tensor_tensor(ln_s[:, 3], ln_s[:, 2], ln_s[:, 2], ALU.mult))
                step(v.tensor_tensor(ln_s[:, 4], ln_s[:, 3], ln_s[:, 0], ALU.mult))
                step(v.tensor_scalar(ln_s[:, 3], ln_s[:, 4], -0.5, 1.5, ALU.mult, ALU.add))
                step(v.tensor_tensor(ln_s[:, 5], ln_s[:, 2], ln_s[:, 3], ALU.mult))
                for n in range(NT):
                    v.tensor_scalar(h[:, n], xs[:, n], mv[:, n, 0:1], ln_s[:, 5, n:n + 1], ALU.subtract,
                                    ALU.mult).then_inc(h_made, 1)

            layer_norm(0, stream)

            def split_at(i, j):
                dve.wait_ge(w_hi_made, i * 3 + j + 1)
                v.tensor_tensor(w_lo[:, j], raw[:, j], w_hi[:, j].bitcast(F32), ALU.subtract).then_inc(w_lo_made, 1)

            split_at(0, 0)

            def compare(cols, n, fetch):
                dve.wait_ge(key_in, fetch * 16 + 16)
                flat = key_bc.rearrange("p a b -> p (a b)")
                for c in range(n):
                    ins = v.scalar_tensor_tensor(out=flat[:, c * P:(c + 1) * P], in0=flat[:, c * P:(c + 1) * P],
                                                 scalar=key_col[:, bass.ds(cols + c, 1)], in1=later[:],
                                                 op0=ALU.is_equal, op1=ALU.mult, accum_out=later_n[:, c:c + 1])
                ins.then_inc(keys_used, 1)
                dve.wait_ge(keys_used, fetch + 1)
                v.scalar_tensor_tensor(out=value[:, 0:n], in0=later_n[:, 0:n], scalar=0.0,
                                       in1=evalue[:, bass.ds(cols, n)], op0=ALU.is_equal,
                                       op1=ALU.mult).then_inc(valued, 1)
                dve.wait_ge(valued, fetch + 1)

            def hot(col, c):
                slot = (c + 1) % 4 if isinstance(col, int) and col < CH0 else c % 4
                wait(dve, hot_used, col - 3)
                v.tensor_scalar(src_hot[:, slot], nodes[:], cols_f[:, 0, bass.ds(col, 1)], None, ALU.is_equal)
                v.tensor_scalar(dst_hot[:, slot], nodes[:], cols_f[:, 1, bass.ds(col, 1)], value[:, c:c + 1],
                                ALU.is_equal, ALU.mult).then_inc(hot_made, 1)

            compare(0, CH0, 0)
            for c in range(CH0):
                hot(c, c)
            for n in range(NT):
                ins = v.tensor_scalar(diag_hot[:, n], nodes[:], tile_row[:, n:n + 1],
                                      2.0 ** (EXP_BASE - 1 - 127), ALU.is_equal, ALU.mult)
            step(ins)
            for ko in range(KO):
                dve.wait_ge(ln_hi, ko + 1)
                v.tensor_tensor(hT_lo[:, ko], bank[ko][:, 0:N], hT_hi[:, ko].bitcast(F32),
                                ALU.subtract).then_inc(ln_lo, 1)
            dve.wait_ge(ew_exp, 1)
            step(v.tensor_scalar(ew_s[:, 3], ew[:], 0.0, None, ALU.max))
            step(v.tensor_tensor(ew_s[:, 4], ew_s[:, 3], ew_s[:, 2], ALU.add))
            step(v.tensor_scalar(ew_s[:, 3], ew_s[:, 4], 8.0, None, ALU.mult))
            dve.wait_ge(const_in, 48)
            v.tensor_reduce(hs[:, 0:1], b1c[:], AX.X, ALU.max, apply_absolute_value=True).then_inc(b1_max, 1)
            dve.wait_ge(b1_all, 1)
            step(v.tensor_scalar(hs[:, 2:3], hs[:, 1:2], H_SUM_MAX, None, ALU.add))
            step(v.tensor_scalar(hsi[:, 0:1], hs[:, 2:3].bitcast(I32), 23, None, ALU.logical_shift_right))
            step(v.tensor_scalar(hsi[:, 1:2], hsi[:, 0:1], -1.0, 268.0, ALU.mult, ALU.add))
            step(v.tensor_scalar(hsi[:, 2:3], hsi[:, 0:1], 14.0, None, ALU.subtract))
            step(v.tensor_scalar(hs[:, 3:4].bitcast(I32), hsi[:, 1:2], 23, None, ALU.logical_shift_left))
            step(v.tensor_scalar(hs[:, 5:6].bitcast(I32), hsi[:, 2:3], 23, None, ALU.logical_shift_left))
            step(v.tensor_scalar(hs[:, 4:5], hs[:, 3:4], 1.0 / H_SCALE, None, ALU.mult))
            step(v.tensor_scalar(b1s[:], b1c[:], hs[:, 3:4], None, ALU.mult))

            def low_of(out_ap, i, j, b):
                dve.wait_ge(proj_hi_made, i * 3 + j + 1)
                return v.scalar_tensor_tensor(out=out_ap[0], in0=bank[BANK_PROJ + j][:, 0:N], scalar=b,
                                              in1=out_ap[1].bitcast(F32), op0=ALU.add, op1=ALU.subtract)

            def stage1(i):
                for j in range(3):
                    split_at(i + (j + 1) // 3, (j + 1) % 3)
                    if j == 0:
                        compare(i * CPI + CH0, CPI, i + 1)
                    for c in range(CPS):
                        hot(i * CPI + (CH0 + CPS * j + c), CPS * j + c)
                    at = bass.ds(i, 1)
                    low_of((qkv_lo[j][:, at, :], qkv_hi[j][:, at, :]), i, j,
                           bias[:, j, at]).then_inc(proj_lo_made, 1)

            def read_group_a():
                dve.wait_ge(group_done, 1)
                for n in range(NT):
                    ins = v.tensor_scalar(expo[:, n], bank[BANK_MASK + n][:, 0:N].bitcast(I32), 23, None,
                                          ALU.logical_shift_right)
                ins.then_inc(group_read, 1)

            stage1(0)
            with dve.Fori(1, 4) as i:
                stage1(i)
            read_group_a()
            with dve.Fori(4, KO) as i:
                stage1(i)

            def make_mask(n):
                if n == 0:
                    dve.wait_ge(group_done, 2)
                    dve.wait_ge(group_read, 1)
                step(v.tensor_scalar(m_i[:, 0], bank[BANK_MASK + n][:, 0:N].bitcast(I32), 23, None,
                                     ALU.logical_shift_right))
                step(v.scalar_tensor_tensor(out=m_i[:, 1], in0=m_i[:, 0], scalar=0.0, in1=expo[:, n],
                                            op0=ALU.is_equal, op1=ALU.mult))
                step(v.tensor_tensor(expo[:, n], m_i[:, 0], m_i[:, 1], ALU.add))
                step(v.tensor_scalar(mask8[:, n], expo[:, n], 0.0, NEG, ALU.is_equal, ALU.mult))
                step(v.tensor_scalar(m_i[:, 0], expo[:, n], ETYPES - 1, None, ALU.bitwise_and))
                for t in range(ETYPES):
                    step(v.tensor_scalar(m_f, m_i[:, 0], float(t), ew_s[:, 3, t:t + 1], ALU.is_equal, ALU.mult))
                    ins = v.tensor_tensor(mask8[:, n], mask8[:, n], m_f, ALU.add)
                    if t < ETYPES - 1:
                        step(ins)
                    else:
                        ins.then_inc(mask_made, 1)

            def stage2(i, project, attend):
                p = i - 1

                def mask_scores(k):
                    dve.wait_ge(scored, p * 6 + k + 1)
                    dve.sem_inc(scores_seen, 1)
                    dve.wait_ge(mask_made, NT)
                    v.tensor_tensor_reduce(probs[:, k], bank[BANK_SCORE + k % 2][:, 0:N], mask8[:, k % NT],
                                           1.0, -3.4e38, ALU.add, ALU.max, sm[:, 0, k:k + 1]).then_inc(score_max, 1)
                    dve.wait_ge(score_max, p * 6 + k + 1)
                    v.tensor_scalar(sm[:, 1, k:k + 1], sm[:, 0, k:k + 1], -0.125, None, ALU.mult).then_inc(max_neg, 1)

                def norm(k):
                    dve.wait_ge(exped, p * 6 + k + 1)
                    v.reciprocal(sm[:, 3, k:k + 1], sm[:, 2, k:k + 1]).then_inc(inv_made, 1)
                    dve.wait_ge(inv_made, p * 6 + k + 1)
                    v.tensor_scalar(probs[:, k], probs[:, k], sm[:, 3, k:k + 1], None, ALU.mult).then_inc(normed, 1)

                def turn(k):
                    at = slice((k % NT) * P, (k % NT + 1) * P)
                    dve.wait_ge(turn_hi, p * 7 + k + 2)
                    v.tensor_tensor(pT_lo[:, :, at],
                                    bank[BANK_TURN + (k + 1) % 2][:, 0:N].rearrange("p (a b) -> p a b", a=NT),
                                    pT_hi[:, :, at].bitcast(F32), ALU.subtract).then_inc(turn_lo, 1)

                def pv_out(h):
                    rows = slice(HD * h, HD * h + HD)
                    dve.wait_ge(pv_hi, p * 2 + h + 1)
                    v.tensor_tensor(hT_lo[rows, bass.ds(p, 1), :], bank[BANK_PV][rows, 0:N],
                                    hT_hi[rows, bass.ds(p, 1), :].bitcast(F32), ALU.subtract).then_inc(pv_lo, 1)

                def project_out(j):
                    low_of(((q2_lo, k2_lo)[j][:], (q2_hi, k2_hi)[j][:]), i + KO, j,
                           bias[:, 3 + j, bass.ds(i, 1)]).then_inc(proj_lo_made, 1)

                if attend:
                    dve.wait_ge(turn_hi, p * 7 + 1)
                    v.tensor_tensor(v2_lo[:].rearrange("p a b -> p (a b)"), bank[BANK_TURN][:, 0:N],
                                    v2_hi[:].rearrange("p a b -> p (a b)").bitcast(F32),
                                    ALU.subtract).then_inc(turn_lo, 1)
                    mask_scores(0)
                    mask_scores(1)
                if project:
                    split_at(i + KO, 1)
                if attend:
                    norm(0)
                    mask_scores(2)
                    norm(1)
                    mask_scores(3)
                    norm(2)
                    mask_scores(4)
                    norm(3)
                    turn(0)
                    mask_scores(5)
                    norm(4)
                    turn(1)
                if project:
                    if not attend:
                        make_mask(0)
                    project_out(0)
                if attend:
                    norm(5)
                    turn(2)
                if project:
                    split_at(i + KO, 2)
                    if not attend:
                        make_mask(1)
                if attend:
                    pv_out(0)
                    turn(3)
                if project:
                    project_out(1)
                    if not attend:
                        make_mask(2)
                if attend:
                    turn(4)
                    turn(5)
                if project:
                    split_at(i + KO + 1, 0)
                if attend:
                    pv_out(1)

            stage2(0, True, False)
            with dve.Fori(1, PAIRS) as i:
                stage2(i, True, True)
            dve.wait_ge(gamma_done, FT)
            for m in range(2):
                ins = v.tensor_reduce(gsum[:, m:m + 1], gacc[:, m * FT // 2:(m + 1) * FT // 2], AX.X, ALU.add)
            ins.then_inc(gsum_made, 1)
            stage2(PAIRS, False, True)
            dve.wait_ge(gsum_all, 1)
            step(v.tensor_scalar(gsum[:], bank[BANK_PROJ][:, 0:2], 1.0 / (F * D), None, ALU.mult))
            step(v.tensor_scalar(thr[:, 0:2], gsum[:], EPS, 0.5, ALU.add, ALU.mult))
            v.tensor_scalar(thr[:, 2:4], thr[:, 0:2], -1.0, None, ALU.mult).then_inc(gsum_all, 1)

            for s in range(stage3, SLABS):
                if s + 1 < SLABS:
                    split_at((s + 1) // 3, (s + 1) % 3)
                m = s - stage3
                dve.wait_ge(o_turned, m + 1)
                at = slice(m * P, (m + 1) * P)
                v.tensor_tensor(xs[:, :, at], xs[:, :, at],
                                bank[BANK_TURN + m % 2][:, 0:N].rearrange("p (a b) -> p a b", a=NT),
                                ALU.add).then_inc(x_added, 1)
            dve.wait_ge(x_added, KO)
            layer_norm(1, raw)
            for ko in range(KO):
                dve.wait_ge(ln_hi, KO + ko + 1)
                v.scalar_tensor_tensor(out=h2_lo[:, ko], in0=bank[ko][:, 0:N], scalar=H_SCALE, in1=h2_hi[:, ko],
                                       op0=ALU.mult, op1=ALU.subtract).then_inc(ln_lo, 1)

            def ternary(t, u):
                for m in range(2):
                    dve.wait_ge(minus_made, t * 2 + m + 1)
                    if m == 0:
                        wait(dve, hid_done, t - 1)
                    else:
                        wait(dve, y_step, t - 1)
                    v.scalar_tensor_tensor(out=tern[:, m, u], in0=stream[:, 2 * m + u], scalar=thr[:, m:m + 1],
                                           in1=minus[:, m, u], op0=ALU.is_gt, op1=ALU.subtract).then_inc(tern_made, 1)

            def act_low(t, u):
                dve.wait_ge(act_hi_made, t + 1)
                v.tensor_tensor(act_lo[:, u], act[:, u], act_hi[:, u], ALU.subtract).then_inc(act_lo_made, 1)

            ternary(0, 0)
            ternary(1, 1)
            act_low(0, 0)
            with dve.Fori(1, FT // 2) as i:
                for u in range(2):
                    ternary(i * 2 + u, u)
                    act_low(i * 2 + (u - 1), (u - 1) % 2)
            act_low(FT - 1, 1)
            dve.wait_ge(b2_added, NT)
            dve.wait_ge(y_done, 1)
            for n in range(NT):
                for c in range(2):
                    at = slice(c * 512, (c + 1) * 512)
                    v.scalar_tensor_tensor(out=xs[:, n, at], in0=bank[BANK_Y + 2 * n + c][:], scalar=hs[:, 5:6],
                                           in1=xs[:, n, at], op0=ALU.mult, op1=ALU.add).then_inc(y_ready, 1)

        @block.tensor
        def _(pe):
            t_ = nc.tensor

            def turn_h(k, h):
                pe.wait_ge(h_made, NT * (k + 1))
                for ko in range(KO):
                    if k == 1 and ko >= BANK_TURN:
                        pe.wait_ge(x_added, KO)
                    for n in range(NT):
                        ins = t_.transpose(bank[ko][:, n * P:(n + 1) * P], h[:, n, ko * P:(ko + 1) * P], ident[:])
                    ins.then_inc(ln_turned, 1)

            pe.wait_ge(consts, 9)
            turn_h(0, stream)
            pe.wait_ge(ln_lo, KO)

            def passes(outp, l_hi, l_lo, r_hi, r_lo, first, last):
                t_.matmul(outp, l_hi, r_hi, start=first, stop=False)
                t_.matmul(outp, l_hi, r_lo, start=False, stop=False)
                return t_.matmul(outp, l_lo, r_hi, start=False, stop=last)

            def project(s, j, r_hi, r_lo, kos):
                if kos[0] == 0:
                    pe.wait_ge(w_lo_made, s + 1)
                for ko in kos:
                    w = slice(ko * P, (ko + 1) * P)
                    ins = passes(bank[BANK_PROJ + j][:, 0:N], w_hi[:, j, w], w_lo[:, j, w], r_hi[:, ko], r_lo[:, ko],
                                 ko == 0, ko == KO - 1)
                if kos[-1] == KO - 1:
                    ins.then_inc(slab_done, 1)

            def scatter(col, c, first=False):
                slot = (c + 1) % 4 if isinstance(col, int) and col < CH0 else c % 4
                pe.wait_ge(hot_made, col + 1)
                for n in range(NT):
                    ins = t_.matmul(bank[BANK_MASK + n][:, 0:N], src_hot[:, slot, n * P:(n + 1) * P],
                                    dst_hot[:, slot], start=first, stop=False)
                ins.then_inc(hot_used, 1)

            def flat_add(table, first, last):
                for n in range(NT):
                    ins = t_.matmul(bank[BANK_MASK + n][:, 0:N], ident_b[:], table(n), start=first, stop=last)
                return ins

            for c in range(CH0):
                scatter(c, c, c == 0)

            def stage1(i):
                for j in range(3):
                    wait(pe, proj_lo_made, i * 3 + j - 2)
                    project(i * 3 + j, j, hT_hi, hT_lo, range(KO))
                    for c in range(CPS):
                        scatter(i * CPI + (CH0 + CPS * j + c), CPS * j + c)

            stage1(0)
            with pe.Fori(1, 4) as i:
                stage1(i)
            flat_add(lambda n: diag_hot[:, n], False, True).then_inc(group_done, 1)
            pe.wait_ge(group_read, 1)
            flat_add(lambda n: zeros_b[:], True, False)
            with pe.Fori(4, KO) as i:
                stage1(i)
            flat_add(lambda n: zeros_b[:], False, True).then_inc(group_done, 1)

            def stage2(i, do_project, attend):
                p = i - 1
                s = (i + KO) * 3

                def proj(j, part):
                    kos = ((0, 1, 2), (3, 4, 5), (6, 7))[part]
                    if do_project:
                        if part == 0 and j < 2:
                            pe.wait_ge(proj_lo_made, i * 2 + (3 * KO - 1 + j))
                        elif part == 0:
                            pe.wait_ge(proj_hi_made, s)
                        project(s + j, j, qkv_hi[j], qkv_lo[j], kos)

                def score(k):
                    h, n = k // NT, k % NT
                    rows = slice(HD * h, HD * h + HD)
                    at = slice(n * P, (n + 1) * P)
                    if not attend:
                        return
                    if k == 0:
                        pe.wait_ge(proj_lo_made, p * 2 + (3 * KO + 2))
                    if k >= 2:
                        pe.wait_ge(score_max, p * 6 + k - 1)
                    passes(bank[BANK_SCORE + k % 2][:, 0:N], q2_hi[rows, at], q2_lo[rows, at],
                           k2_hi[rows], k2_lo[rows], True, True).then_inc(scored, 1)

                def turn_v():
                    if not attend:
                        return
                    pe.wait_ge(proj_hi_made, s)
                    for n in range(NT):
                        at = slice(n * P, (n + 1) * P)
                        ins = t_.transpose(bank[BANK_TURN][:, at], v2T[:, at], ident[:])
                    ins.then_inc(turned_done, 1)

                def turn(k):
                    if not attend:
                        return
                    pe.wait_ge(normed, p * 6 + k + 1)
                    if k >= 1:
                        pe.wait_ge(turn_lo, p * 7 + k)
                    for n in range(NT):
                        ins = t_.transpose(bank[BANK_TURN + (k + 1) % 2][:, n * P:(n + 1) * P],
                                           probs[:, k, n * P:(n + 1) * P], ident[:])
                    ins.then_inc(turned_done, 1)

                def pv(h):
                    if not attend:
                        return
                    pe.wait_ge(turn_lo, p * 7 + 1 + NT * (h + 1))
                    pe.wait_ge(pv_lo, p * 2 + h + 1)
                    for m in range(NT):
                        ins = passes(bank[BANK_PV][:, 0:N], v2_hi[:, m], v2_lo[:, m], pT_hi[:, m], pT_lo[:, m],
                                     m == 0, m == NT - 1)
                    ins.then_inc(pv_done, 1)

                turn_v()
                score(0)
                score(1)
                proj(0, 0)
                score(2)
                score(3)
                proj(0, 1)
                score(4)
                turn(0)
                proj(0, 2)
                score(5)
                turn(1)
                proj(1, 0)
                turn(2)
                proj(1, 1)
                pv(0)
                turn(3)
                proj(1, 2)
                turn(4)
                proj(2, 0)
                turn(5)
                proj(2, 1)
                proj(2, 2)
                pv(1)

            stage2(0, True, False)
            pe.wait_ge(mask_made, NT)
            with pe.Fori(1, PAIRS) as i:
                stage2(i, True, True)
            pe.wait_ge(gsum_made, 1)
            pe.wait_ge(proj_lo_made, 3 * KO + 2 * PAIRS - 1)
            t_.matmul(bank[BANK_PROJ][:, 0:2], ones[:], gsum[:], start=True, stop=True).then_inc(gsum_all, 1)
            stage2(PAIRS, False, True)
            pe.wait_ge(pv_lo, 2 * PAIRS + 1)
            pe.wait_ge(gsum_all, 2)

            def turn_o(m):
                pe.wait_ge(o_biased, m + 1)
                wait(pe, x_added, m - 1)
                if m < 2:
                    pe.wait_ge(turn_lo, 7 * PAIRS)
                for n in range(NT):
                    at = slice(n * P, (n + 1) * P)
                    ins = t_.transpose(bank[BANK_TURN + m % 2][:, at], turned[:, at], ident[:])
                ins.then_inc(o_turned, 1)

            for s in range(stage3, SLABS):
                m = s - stage3
                j = s % 3
                pe.wait_ge(w_lo_made, s + 1)
                wait(pe, o_biased, m - 2)
                for ko in range(KO):
                    w = slice(ko * P, (ko + 1) * P)
                    ins = passes(bank[BANK_PROJ + j][:, 0:N], w_hi[:, j, w], w_lo[:, j, w], hT_hi[:, ko], hT_lo[:, ko],
                                 ko == 0, ko == KO - 1)
                ins.then_inc(slab_done, 1)
                if m:
                    turn_o(m - 1)
            turn_o(KO - 1)

            turn_h(1, raw)
            pe.wait_ge(ln_lo, 2 * KO)

            def hidden(t, u):
                pe.wait_ge(tern_made, t * 2 + 1)
                wait(pe, relu_done, t - 1)
                for ko in range(KO):
                    for part, h in enumerate((h2_hi, h2_lo)):
                        ins = t_.matmul(bank[BANK_HID + u][:, 0:N], tern[:, 0, u, ko * P:(ko + 1) * P], h[:, ko],
                                        start=(ko == 0 and part == 0), stop=(ko == KO - 1 and part == 1))
                ins.then_inc(hid_done, 1)

            def output(t, u, first=False, last=False):
                pe.wait_ge(tern_made, t * 2 + 2)
                pe.wait_ge(act_lo_made, t + 1)
                for n in range(NT):
                    for part, h in enumerate((act_hi, act_lo)):
                        for c in range(2):
                            ins = t_.matmul(bank[BANK_Y + 2 * n + c][:], h[:, u, n * P:(n + 1) * P],
                                            tern[:, 1, u, c * 512:(c + 1) * 512],
                                            start=first and part == 0, stop=last and part == 1)
                return ins.then_inc(y_step, 1)

            hidden(0, 0)
            hidden(1, 1)
            output(0, 0, first=True)
            with pe.Fori(1, FT // 2) as i:
                for u in range(2):
                    hidden(i * 2 + u, u)
                    output(i * 2 + (u - 1), (u - 1) % 2)
            output(FT - 1, 1, last=True)
            pe.wait_ge(y_step, FT)
            pe.sem_inc(y_done, 1)


def kernel(x, src, dst, edge_type_5, L0_gnn_edge_type_weights, L0_gnn_wq, L0_gnn_bq, L0_gnn_wk, L0_gnn_bk,
           L0_gnn_wv, L0_gnn_bv, L0_gnn_wiq, L0_gnn_biq, L0_gnn_wik, L0_gnn_bik, L0_gnn_wiv, L0_gnn_biv,
           L0_gnn_wo, L0_gnn_bo, L0_ffn_W1, L0_ffn_b1, L0_ffn_W2, L0_ffn_b2):
    import numpy as np
    import concourse.bacc as bacc
    from concourse.bass_utils import run_bass_kernel_spmd

    def slabs(w):
        w = np.asarray(w)
        o, i = w.shape
        return w.reshape(o // P, P, i // P, P).transpose(0, 3, 2, 1).reshape(o // P, P, i)

    def turns(*ws):
        s = np.stack([slabs(w) for w in ws], axis=1)
        return s.reshape(-1, P, D)

    def columns(a):
        return np.ascontiguousarray(np.asarray(a).reshape(-1, P).T)

    w_slabs = np.concatenate([turns(L0_gnn_wq, L0_gnn_wk, L0_gnn_wv),
                              turns(L0_gnn_wiq, L0_gnn_wik, L0_gnn_wiv), slabs(L0_gnn_wo)])
    biases = np.stack([columns(b) for b in (L0_gnn_bq, L0_gnn_bk, L0_gnn_bv, L0_gnn_biq, L0_gnn_bik, L0_gnn_biv,
                                            L0_gnn_bo)], axis=1)
    ffn_slabs = np.concatenate([slabs(L0_ffn_W1), np.asarray(L0_ffn_W2).T.reshape(FT, P, D)])
    arrays = {
        "x": np.asarray(x),
        "src_rows": np.asarray(src).reshape(CH, P), "dst_rows": np.asarray(dst).reshape(CH, P),
        "src_cols": columns(src), "dst_cols": columns(dst), "type_cols": columns(edge_type_5),
        "edge_w": np.asarray(L0_gnn_edge_type_weights),
        "w_slabs": w_slabs, "biases": biases, "ffn_slabs": ffn_slabs,
        "b1": columns(L0_ffn_b1), "b2": np.asarray(L0_ffn_b2),
    }
    arrays = {f"in_{k}": np.ascontiguousarray(v) for k, v in arrays.items()}
    nc = bacc.Bacc("TRN2", target_bir_lowering=False, num_devices=1)
    args = [nc.dram_tensor(k, v.shape, mybir.dt.from_np(v.dtype), kind="ExternalInput").ap() for k, v in arrays.items()]
    out = nc.dram_tensor("out", (N, D), F32, kind="ExternalOutput").ap()
    gnn_ffn_kernel(nc, *args, out)
    r = run_bass_kernel_spmd(nc, [arrays], core_ids=[0])
    return r.results[0]["out"]
```

```python
from contextlib import ExitStack

import concourse.bass as bass
from concourse import mybir

F32 = mybir.dt.float32
F32R = mybir.dt.float32r
BF16 = mybir.dt.bfloat16
F16 = mybir.dt.float16
I32 = mybir.dt.int32
ALU = mybir.AluOpType
ACT = mybir.ActivationFunctionType
AX = mybir.AxisListType

P = 128
N = 384
NT = N // P
D = 1024
KO = D // P
HD = 64
PAIRS = D // (2 * HD)
F = 4 * D
FT = F // P
E = 12672
CH = E // P
CPI = 16
CPI0 = 3
SPLIT = (range(0, 8), range(8, 12), range(12, 16))
GROUP_A = CPI0 + 3 * CPI
AHEAD = range(3, 6)
ETYPES = 4
EPS = 1e-5
NEG = -3.0e38
EXP_BASE = 20
SLABS = 56
H_SCALE = 1024.0
H_SUM_MAX = 1024.0

BANK_PROJ, BANK_SCORE, BANK_TURN, BANK_PV = 0, 3, 5, 7
BANK_MASK = 3
BANK_HID, BANK_Y = 0, 2

Y_PARTS = [(n, c) for n in range(NT) for c in range(2)]
Y_BY_POOL = ((0, 1), (1, 1))
Y_ORDER = (0, 2, 1, 4, 3, 5)


def wait(eng, sem, value):
    if not (isinstance(value, int) and value <= 0):
        eng.wait_ge(sem, value)


def gnn_ffn_kernel(nc, x, edge_rows, edge_cols, edge_w, w_slabs, biases,
                   ffn_slabs, b1, b2, out):
    ctx = ExitStack()
    early, edges, pairs = ExitStack(), ExitStack(), ExitStack()
    late = ExitStack()
    with ctx:
        def sb(name, shape, dt, scope=ctx):
            return scope.enter_context(nc.sbuf_tensor(name, shape, dt))

        def sem(name):
            return ctx.enter_context(nc.semaphore(name))

        xs = sb("xs", [P, NT, D], F32)
        raw = sb("raw", [P, 3, D], F32)
        w_hi = sb("w_hi", [P, 3, D], F32R)
        w_lo = sb("w_lo", [P, 3, D], F32R)
        hT_hi = sb("hT_hi", [P, KO, N], F32R)
        hT_lo = sb("hT_lo", [P, KO, N], F32R)
        stream = sb("stream", [P, 4, D], F32)
        bias = sb("bias", [P, 7, KO], F32)
        b1c = sb("b1c", [P, FT], F32)
        b1s = sb("b1s", [P, FT], F32)
        ident = sb("ident", [P, P], F32)
        ones = sb("ones", [P, P], F32)
        stats = sb("stats", [P, NT, KO, 6], F32)
        mv = sb("mv", [P, NT, 2], F32)
        ln_s = sb("ln_s", [P, 6, NT], F32)
        gacc = sb("gacc", [P, 2 * FT // 2], F32)
        gsum = sb("gsum", [P, 2], F32)
        thr = sb("thr", [P, 2], F32)
        hs = sb("hs", [P, 8], F32)
        hsi = sb("hsi", [P, 4], I32)
        qkv_hi = [sb(f"qkv_hi{j}", [P, KO, N], F32R, early) for j in range(3)]
        qkv_lo = [sb(f"qkv_lo{j}", [P, KO, N], F32R, early) for j in range(3)]
        mask8 = sb("mask8", [P, NT, N], F32, early)
        probs = sb("probs", [P, 6, N], F32, early)
        sm = sb("sm", [P, 4, 6], F32, early)
        ew = sb("ew", [P, ETYPES], F32, early)
        ew_s = sb("ew_s", [P, 5, ETYPES], F32, early)
        src_hot = sb("src_hot", [P, 4, N], BF16, edges)
        dst_hot = sb("dst_hot", [P, 4, N], BF16, edges)
        nodes = sb("nodes", [P, N], F16, edges)
        later = sb("later", [P, P], F32, edges)
        ident_b = sb("ident_b", [P, P], BF16, edges)
        diag_hot = sb("diag_hot", [P, NT, N], BF16, edges)
        zeros_b = sb("zeros_b", [P, N], BF16, edges)
        tile_row = sb("tile_row", [P, NT], F32, edges)
        rows_i = sb("rows_i", [CH, 2, P], I32, edges)
        key_rows = sb("key_rows", [CH, P], F32, edges)
        cols_i = sb("cols_i", [P, 3, CH], I32, edges)
        cols_f = sb("cols_f", [P, 2, CH], F32, edges)
        key_col = sb("key_col", [P, CH], F32, edges)
        expo = sb("expo", [P, NT, N], I32, edges)
        ebase = sb("ebase", [P, CH], I32, edges)
        etmp = sb("etmp", [P, 2, CH], I32, edges)
        later_n = sb("later_n", [P, CPI], F32, edges)
        value = sb("value", [P, CPI], F32, edges)
        edges.close()
        q2_hi = sb("q2_hi", [P, N], F32R, pairs)
        q2_lo = sb("q2_lo", [P, N], F32R, pairs)
        k2_hi = sb("k2_hi", [P, N], F32R, pairs)
        k2_lo = sb("k2_lo", [P, N], F32R, pairs)
        v2T = sb("v2T", [P, N], F32, pairs)
        v2_hi = sb("v2_hi", [P, NT, P], F32R, pairs)
        v2_lo = sb("v2_lo", [P, NT, P], F32R, pairs)
        pT_hi = [sb(f"pT_hi{h}", [P, NT, N], F32R, pairs) for h in range(2)]
        pT_lo = [sb(f"pT_lo{h}", [P, NT, N], F32R, pairs) for h in range(2)]
        pairs.close()
        early.close()
        b2r = sb("b2r", [P, D], F32, late)
        turned = sb("turned", [P, N], F32, late)
        h2_hi = sb("h2_hi", [P, KO, N], F16, late)
        h2_lo = sb("h2_lo", [P, KO, N], F16, late)
        sgn = sb("sgn", [P, 2, 2, D], F16, late)
        tern = sb("tern", [P, 2, 2, D], F16, late)
        act = sb("act", [P, 2, N], F32, late)
        act_hi = sb("act_hi", [P, 2, N], F16, late)
        act_lo = sb("act_lo", [P, 2, N], F16, late)
        late.close()
        bank = [ctx.enter_context(nc.psum_tensor(f"bank{i}", [P, 512], F32)) for i in range(8)]
        key_dram = nc.dram_tensor("key_scratch", [CH * P], F32, kind="Internal").ap()
        bits = [probs[:, 2 * n].bitcast(I32) for n in range(NT)]
        m_f = [probs[:, 2 * n + 1] for n in range(NT)]
        first_keys = mask8[:, 0]
        key_bc = probs[:, 0:6, :]

        x_in = [sem(f"x_in{n}") for n in range(NT)]
        edges_in, const_in, rows_in = sem("edges_in"), sem("const_in"), sem("rows_in")
        raw_in = [sem(f"raw_in{j}") for j in range(3)]
        key_out, first_key_in, key_in = sem("key_out"), sem("first_key_in"), sem("key_in")
        gamma_in = [sem(f"gamma_in{u}") for u in range(2)]
        consts = sem("consts")
        key_made = sem("key_made")
        pre = sem("pre")
        a_pre = sem("a_pre")
        w_hi_made, w_lo_made, slab_done = sem("w_hi_made"), sem("w_lo_made"), sem("slab_done")
        proj_hi_made, proj_lo_made = sem("proj_hi_made"), sem("proj_lo_made")
        ln_turned, ln_hi, ln_lo = sem("ln_turned"), sem("ln_hi"), sem("ln_lo")
        var_made, sd_made = sem("var_made"), sem("sd_made")
        h_made = sem("h_made")
        gamma_done = sem("gamma_done")
        keys_used, counted, valued = sem("keys_used"), sem("counted"), sem("valued")
        hot_made, hot_used = sem("hot_made"), sem("hot_used")
        group_done, group_read = sem("group_done"), sem("group_read")
        ew_exp = sem("ew_exp")
        mask_made = [sem(f"mask_made{n}") for n in range(NT)]
        scored, score_max, max_neg, exped, inv_made, normed = (
            sem("scored"), sem("score_max"), sem("max_neg"), sem("exped"), sem("inv_made"), sem("normed"))
        turned_done, turn_hi, turn_lo = sem("turned_done"), sem("turn_hi"), sem("turn_lo")
        pv_done, pv_hi, pv_lo = sem("pv_done"), sem("pv_hi"), sem("pv_lo")
        gsum_made, gsum_all = sem("gsum_made"), sem("gsum_all")
        o_biased, o_turned, x_added = sem("o_biased"), sem("o_turned"), sem("x_added")
        b1_max, b1_all = sem("b1_max"), sem("b1_all")
        ffn_in = [[sem(f"ffn_in{m}{u}") for u in range(2)] for m in range(2)]
        sgn_made, tern_made = sem("sgn_made"), sem("tern_made")
        hid_done, relu_done, act_hi_made, act_lo_made = sem("hid_done"), sem("relu_done"), sem("act_hi_made"), sem("act_lo_made")
        y_step, y_done, y_scaled, out_done = sem("y_step"), sem("y_done"), sem("y_scaled"), sem("out_done")
        y_ready = [sem(f"y_ready{k}") for k in range(len(Y_PARTS))]
        b2_in = sem("b2_in")
        b2_added, diag_made = sem("b2_added"), sem("diag_made")
        scores_seen = sem("scores_seen")
        bits_read, coded = sem("bits_read"), sem("coded")
        p_pre = sem("p_pre")

        block = ctx.enter_context(nc.Block())
        stage3 = 2 * PAIRS * 3

        @block.sync
        def _(sp):
            for n in range(NT):
                sp.dma_start(xs[:, n], x[n * P:(n + 1) * P]).then_inc(x_in[n], 16)
            sp.wait_ge(key_made, 1)
            sp.dma_start(key_dram.rearrange("(c p) -> c p", p=P), key_rows[:]).then_inc(key_out, 16)
            sp.dma_start(raw[:, 0], w_slabs[0]).then_inc(raw_in[0], 16)
            sp.wait_ge(key_out, 16)
            sp.dma_start(first_keys[:, 0:CPI0 * P],
                         key_dram[0:CPI0 * P].partition_broadcast(P)).then_inc(first_key_in, 16)
            for j in range(1, 3):
                sp.dma_start(raw[:, j], w_slabs[j]).then_inc(raw_in[j], 16)
            flat_keys = key_bc.rearrange("p a b -> p (a b)")
            sp.dma_start(flat_keys[:, 0:CPI * P],
                         key_dram[CPI0 * P:(CPI0 + CPI) * P].partition_broadcast(P)).then_inc(key_in, 16)
            sp.dma_start(b1c[:], b1).then_inc(const_in, 16)

            def fetch_keys(b):
                sp.wait_ge(keys_used, b)
                sp.dma_start(flat_keys[:, 0:CPI * P],
                             key_dram[bass.ds(b * (CPI * P) + (CPI0 - CPI) * P, CPI * P)].partition_broadcast(P)
                             ).then_inc(key_in, 16)

            def fetch_slab(s, j):
                wait(sp, w_lo_made, s - 2)
                sp.dma_start(raw[:, j], w_slabs[s]).then_inc(raw_in[j], 16)

            def fetch_gamma(g, u):
                if isinstance(g, int) and g < 2:
                    sp.wait_ge(ln_turned, KO)
                else:
                    sp.wait_ge(gamma_done, g - 1)
                sp.dma_start(stream[:, 2 * u:2 * u + 2],
                             ffn_slabs[bass.ds(g * 2, 2)].rearrange("t p c -> p t c")).then_inc(gamma_in[u], 16)

            def iteration(i):
                fetch_gamma(i * 2, 0)
                fetch_slab(i * 3 + 3, 0)
                fetch_slab(i * 3 + 4, 1)
                fetch_gamma(i * 2 + 1, 1)
                fetch_slab(i * 3 + 5, 2)

            iteration(0)
            with sp.Fori(1, KO - 2) as i:
                fetch_keys(i + 1)
                iteration(i)
            with sp.Fori(KO - 2, KO + PAIRS) as i:
                iteration(i)
            fetch_slab(stage3 + 3, 0)
            fetch_slab(stage3 + 4, 1)
            fetch_slab(stage3 + 5, 2)
            fetch_slab(stage3 + 6, 0)
            fetch_slab(stage3 + 7, 1)

            sp.wait_ge(slab_done, stage3)
            sp.dma_start(b2r[:], b2.partition_broadcast(P)).then_inc(b2_in, 16)

            def fetch_ffn(t, u):
                for m in range(2):
                    if isinstance(t, int) and t < 2:
                        sp.wait_ge(gamma_done, FT)
                    else:
                        sp.wait_ge(tern_made, t * 2 + m - 3)
                    sp.dma_start(stream[:, 2 * m + u], ffn_slabs[t + m * FT]).then_inc(ffn_in[m][u], 16)

            for u in range(2):
                fetch_ffn(u, u)
            with sp.Fori(1, FT // 2) as i:
                for u in range(2):
                    fetch_ffn(i * 2 + u, u)
            for k in Y_ORDER:
                n, c = Y_PARTS[k]
                sp.wait_ge(y_ready[k], 1)
                sp.dma_start(out[n * P:(n + 1) * P, c * 512:(c + 1) * 512],
                             xs[:, n, c * 512:(c + 1) * 512]).then_inc(out_done, 16)
            sp.wait_ge(out_done, 16 * len(Y_PARTS))

        @block.gpsimd
        def _(pool):
            g = nc.gpsimd
            g.memset(ones[:], 1.0).then_inc(consts, 1)
            g.memset(zeros_b[:], 0.0).then_inc(consts, 1)
            pool.wait_ge(consts, 2)
            g.affine_select(out=ident[:], in_=ones[:], compare_op=ALU.is_equal, fill=0.0, base=0,
                            pattern=[[1, P]], channel_multiplier=-1).then_inc(consts, 1)
            g.affine_select(out=later[:], in_=ones[:], compare_op=ALU.is_gt, fill=0.0, base=0,
                            pattern=[[1, P]], channel_multiplier=-1).then_inc(consts, 1)
            g.iota(nodes[:], [[1, N]], base=0, channel_multiplier=0,
                   allow_small_or_imprecise_dtypes=True).then_inc(consts, 1)
            g.iota(tile_row[:], [[P, NT]], base=0, channel_multiplier=1,
                   allow_small_or_imprecise_dtypes=True).then_inc(consts, 1)
            g.iota(ebase[:, 0:GROUP_A], [[ETYPES, GROUP_A]], base=EXP_BASE, channel_multiplier=0).then_inc(consts, 1)
            g.iota(ebase[:, GROUP_A:CH], [[ETYPES, CH - GROUP_A]], base=EXP_BASE,
                   channel_multiplier=0).then_inc(consts, 1)
            pool.wait_ge(consts, 8)
            g.tensor_copy(ident_b[:], ident[:]).then_inc(consts, 1)

            for j in range(3):
                pool.wait_ge(w_hi_made, j + 1)
                g.tensor_tensor(w_lo[:, j], raw[:, j], w_hi[:, j].bitcast(F32), ALU.subtract).then_inc(w_lo_made, 1)

            pool.wait_ge(b1_max, 1)
            g.partition_all_reduce(hs[:, 1:2], hs[:, 0:1], P, bass.bass_isa.ReduceOp.max).then_inc(b1_all, 1)

            pcount = [0]

            def step(ins):
                pcount[0] += 1
                ins.then_inc(p_pre, 1)
                pool.wait_ge(p_pre, pcount[0])

            pool.wait_ge(coded, NT)
            for n in range(1, NT):
                step(g.tensor_scalar(mask8[:, n], expo[:, n], 0.0, NEG, ALU.is_equal, ALU.mult))
            for n in range(1, NT):
                for t in range(ETYPES):
                    step(g.tensor_scalar(m_f[n], bits[n], float(t), ew_s[:, 3, t:t + 1], ALU.is_equal, ALU.mult))
                    ins = g.tensor_tensor(mask8[:, n], mask8[:, n], m_f[n], ALU.add)
                    if t < ETYPES - 1:
                        step(ins)
                    else:
                        ins.then_inc(mask_made[n], 1)

            pool.wait_ge(b2_in, 16)
            pool.wait_ge(h_made, 4 * NT)
            for n in range(NT):
                g.tensor_tensor(xs[:, n], xs[:, n], b2r[:], ALU.add).then_inc(b2_added, 1)
            pool.wait_ge(b2_added, NT)
            for i, (n, c) in enumerate(Y_BY_POOL):
                at = slice(c * 512, (c + 1) * 512)
                pool.wait_ge(y_scaled, i + 1)
                g.tensor_tensor(xs[:, n, at], xs[:, n, at], raw[:, n, at],
                                ALU.add).then_inc(y_ready[Y_PARTS.index((n, c))], 1)

        @block.scalar
        def _(eng):
            a = nc.scalar
            count = [0]

            def step(ins):
                count[0] += 1
                ins.then_inc(a_pre, 1)
                eng.wait_ge(a_pre, count[0])

            eng.dma_start(rows_i[:], edge_rows).then_inc(rows_in, 16)
            eng.dma_start(cols_i[:], edge_cols).then_inc(edges_in, 16)
            eng.dma_start(ew[:], edge_w.partition_broadcast(P)).then_inc(edges_in, 16)
            eng.dma_start(bias[:], biases).then_inc(const_in, 16)
            eng.wait_ge(edges_in, 32)
            step(a.activation(ew_s[:, 0], ew[:], ACT.Abs))
            step(a.activation(ew_s[:, 1], ew_s[:, 0], ACT.Exp, scale=-1.0))
            step(a.activation(ew_s[:, 2], ew_s[:, 1], ACT.Ln, bias=1.0))
            step(a.activation(ew_s[:, 4], ew_s[:, 0], ACT.Sqrt))

            def root(k):
                eng.wait_ge(var_made, k + 1)
                a.activation(ln_s[:, 1], ln_s[:, 0], ACT.Sqrt, scale=0.25).then_inc(sd_made, 1)

            root(0)

            def split_at(i, j):
                eng.wait_ge(raw_in[j], i * 16 + 16)
                wait(eng, slab_done, i * 3 + j - 2)
                a.activation(w_hi[:, j], raw[:, j], ACT.Copy).then_inc(w_hi_made, 1)

            split_at(0, 0)
            split_at(0, 1)
            split_at(0, 2)
            a.activation(ew_s[:, 4], ew_s[:, 0], ACT.Exp, scale=-1.0).then_inc(ew_exp, 1)
            for ko in range(KO):
                eng.wait_ge(ln_turned, ko + 1)
                a.activation(hT_hi[:, ko], bank[ko][:, 0:N], ACT.Copy).then_inc(ln_hi, 1)

            def magnitudes(g, u):
                eng.wait_ge(gamma_in[u], (g // 2 + 1) * 16 if isinstance(g, int) else g * 8 + 16 - 8 * u)
                flat = stream[:, 2 * u:2 * u + 2].rearrange("p a b -> p (a b)")
                a.activation(flat, flat, ACT.Abs,
                             accum_out=gacc[:, bass.ds(g, 1)]).then_inc(gamma_done, 1)

            eng.wait_ge(const_in, 32)

            def stage1(i):
                for j in range(3):
                    if not isinstance(i, int) or j:
                        split_at(i + (j + 2) // 3, (j + 2) % 3)
                    if j == 0 or j == 1 and not isinstance(i, int):
                        magnitudes(i * 2 + j, j)
                    eng.wait_ge(slab_done, i * 3 + j + 1)
                    a.activation(qkv_hi[j][:, bass.ds(i, 1), :], bank[BANK_PROJ + j][:, 0:N], ACT.Identity,
                                 bias=bias[:, j, bass.ds(i, 1)]).then_inc(proj_hi_made, 1)

            stage1(0)
            magnitudes(1, 1)
            with eng.Fori(1, KO) as i:
                stage1(i)

            def stage2(i, project, attend):
                p = i - 1
                s = (i + KO) * 3

                def exp(k):
                    eng.wait_ge(max_neg, p * 6 + k + 1)
                    a.activation(probs[:, k], probs[:, k], ACT.Exp, bias=sm[:, 1, k:k + 1], scale=0.125,
                                 accum_out=sm[:, 2, k:k + 1]).then_inc(exped, 1)

                def turn(k):
                    n, h = k // 2, k % 2
                    eng.wait_ge(turned_done, p * 7 + k + 2)
                    a.activation(pT_hi[h][:, :, n * P:(n + 1) * P],
                                 bank[BANK_TURN + (k + 1) % 2][:, 0:N].rearrange("p (a b) -> p a b", a=NT),
                                 ACT.Copy).then_inc(turn_hi, 1)

                def pv_out(h):
                    rows = slice(HD * h, HD * h + HD)
                    eng.wait_ge(pv_done, p * 2 + h + 1)
                    a.activation(hT_hi[rows, bass.ds(p, 1), :], bank[BANK_PV][rows, 0:N],
                                 ACT.Copy).then_inc(pv_hi, 1)

                def project_out(j):
                    eng.wait_ge(slab_done, s + j + 1)
                    if j < 2:
                        wait(eng, scored, p * 6 + 6)
                        a.activation((q2_hi, k2_hi)[j][:], bank[BANK_PROJ + j][:, 0:N], ACT.Identity,
                                     bias=bias[:, 3 + j, bass.ds(i, 1)]).then_inc(proj_hi_made, 1)
                    else:
                        a.activation(v2T[:], bank[BANK_PROJ + j][:, 0:N], ACT.Identity,
                                     bias=bias[:, 3 + j, bass.ds(i, 1)]).then_inc(proj_hi_made, 1)

                def turn_v():
                    eng.wait_ge(turned_done, p * 7 + 1)
                    a.activation(v2_hi[:].rearrange("p a b -> p (a b)"), bank[BANK_TURN][:, 0:N],
                                 ACT.Copy).then_inc(turn_hi, 1)

                if attend:
                    exp(0)
                    exp(1)
                    turn_v()
                    exp(2)
                    exp(3)
                    turn(0)
                    turn(1)
                if project or i == PAIRS:
                    split_at(i + KO, 2)
                if attend:
                    turn(2)
                    exp(4)
                if project:
                    project_out(0)
                if attend:
                    exp(5)
                    turn(3)
                    turn(4)
                if project:
                    project_out(1)
                if attend:
                    turn(5)
                if project:
                    split_at(i + KO + 1, 0)
                if attend:
                    pv_out(0)
                if project:
                    split_at(i + KO + 1, 1)
                    magnitudes((i + KO) * 2, 0)
                if attend:
                    pv_out(1)
                if project:
                    magnitudes((i + KO) * 2 + 1, 1)
                    project_out(2)

            stage2(0, True, False)
            with eng.Fori(1, PAIRS) as i:
                stage2(i, True, True)
            stage2(PAIRS, False, True)

            def stage3_step(s, j):
                m = s - stage3
                if s + 3 < SLABS:
                    split_at(s // 3 + 1, j)
                eng.wait_ge(slab_done, s + 1)
                wait(eng, o_turned, m)
                a.activation(turned[:], bank[BANK_PROJ + j][:, 0:N], ACT.Identity,
                             bias=bias[:, 6, m:m + 1]).then_inc(o_biased, 1)

            def signs(t, u, m):
                eng.wait_ge(ffn_in[m][u], (t // 2 + 1) * 16 if isinstance(t, int) else t * 8 + 16 - 8 * u)
                wait(eng, tern_made, t * 2 + m - 3)
                a.activation(sgn[:, m, u], stream[:, 2 * m + u], ACT.Sign, bias=thr[:, m:m + 1]).then_inc(sgn_made, 1)

            for s in range(stage3, SLABS):
                stage3_step(s, s % 3)
                if s - stage3 in AHEAD:
                    k = s - stage3 - AHEAD[0]
                    if k == 0:
                        eng.wait_ge(gsum_all, 2)
                    signs(k // 2, k // 2, k % 2)

            root(1)
            for ko in range(KO):
                eng.wait_ge(ln_turned, KO + ko + 1)
                a.activation(h2_hi[:, ko], bank[ko][:, 0:N], ACT.Copy, scale=H_SCALE).then_inc(ln_hi, 1)
            signs(1, 1, 1)

            def relu(t, u):
                eng.wait_ge(hid_done, t + 1)
                wait(eng, act_lo_made, t - 1)
                a.activation(act[:, u], bank[BANK_HID + u][:, 0:N], ACT.Relu, bias=b1s[:, bass.ds(t, 1)],
                             scale=hs[:, 4:5]).then_inc(relu_done, 1)
                eng.wait_ge(relu_done, t + 1)
                wait(eng, y_step, t - 1)
                a.activation(act_hi[:, u], act[:, u], ACT.Copy).then_inc(act_hi_made, 1)

            relu(0, 0)
            with eng.Fori(1, FT // 2) as i:
                for u in range(2):
                    signs(i * 2 + u, u, 0)
                    relu(i * 2 + (u - 1), (u - 1) % 2)
                    signs(i * 2 + u, u, 1)
            relu(FT - 1, 1)
            for k, (n, c) in enumerate(Y_PARTS):
                if (n, c) in Y_BY_POOL:
                    eng.wait_ge(y_done, k + 1)
                    eng.wait_ge(h_made, 4 * NT)
                    a.activation(raw[:, n, c * 512:(c + 1) * 512], bank[BANK_Y + 2 * n + c][:], ACT.Copy,
                                 scale=hs[:, 5:6]).then_inc(y_scaled, 1)

        @block.vector
        def _(dve):
            v = nc.vector
            count = [0]

            def step(ins):
                count[0] += 1
                ins.then_inc(pre, 1)
                dve.wait_ge(pre, count[0])

            dve.sem_inc(pv_lo, 1)
            dve.wait_ge(rows_in, 16)
            v.scalar_tensor_tensor(out=key_rows[:], in0=rows_i[:, 0], scalar=float(N), in1=rows_i[:, 1],
                                   op0=ALU.mult, op1=ALU.add).then_inc(key_made, 1)
            evalue = etmp[:, 1].bitcast(F32)

            def edge_values():
                dve.wait_ge(consts, 9)
                dve.wait_ge(edges_in, 32)
                v.tensor_copy(cols_f[:], cols_i[:, 0:2])
                step(v.scalar_tensor_tensor(out=key_col[:], in0=cols_i[:, 0], scalar=float(N), in1=cols_i[:, 1],
                                            op0=ALU.mult, op1=ALU.add))
                step(v.tensor_scalar(etmp[:, 0], cols_i[:, 2], float(ETYPES - 1), None, ALU.add))
                step(v.tensor_scalar(etmp[:, 1], etmp[:, 0], ETYPES - 1, None, ALU.bitwise_and))
                step(v.tensor_tensor(etmp[:, 0], etmp[:, 1], ebase[:], ALU.add))
                step(v.tensor_scalar(etmp[:, 1], etmp[:, 0], 23, None, ALU.logical_shift_left))

            def layer_norm(k, h):
                for n in range(NT):
                    if k == 0:
                        dve.wait_ge(x_in[n], 16)
                        for c in range(2):
                            step(v.bn_stats(stats[:, n, c], xs[:, n, c * 512:(c + 1) * 512]))
                    ins = v.bn_aggr(mv[:, n], stats[:, n, 0:2] if k == 0 else stats[:, n])
                step(ins)
                v.tensor_scalar(ln_s[:, 0], mv[:, :, 1], EPS, None, ALU.add).then_inc(var_made, 1)
                dve.wait_ge(sd_made, k + 1)
                step(v.reciprocal(ln_s[:, 2], ln_s[:, 1]))
                step(v.tensor_tensor(ln_s[:, 3], ln_s[:, 2], ln_s[:, 0], ALU.mult))
                step(v.scalar_tensor_tensor(out=ln_s[:, 4], in0=ln_s[:, 3], scalar=0.25, in1=ln_s[:, 1],
                                            op0=ALU.mult, op1=ALU.add))
                step(v.reciprocal(ln_s[:, 5], ln_s[:, 4]))
                for half in range(2):
                    at = slice(half * D // 2, (half + 1) * D // 2)
                    for n in range(NT):
                        v.tensor_scalar(h[:, n, at], xs[:, n, at], mv[:, n, 0:1], ln_s[:, 5, n:n + 1], ALU.subtract,
                                        ALU.mult).then_inc(h_made, 1)

            layer_norm(0, stream)
            edge_values()

            def split_at(i, j):
                dve.wait_ge(w_hi_made, i * 3 + j + 1)
                v.tensor_tensor(w_lo[:, j], raw[:, j], w_hi[:, j].bitcast(F32), ALU.subtract).then_inc(w_lo_made, 1)

            def compare(cols, chunks, n, fetch):
                flat = key_bc.rearrange("p a b -> p (a b)") if n == CPI else first_keys
                if n == CPI0:
                    dve.wait_ge(first_key_in, 16)
                elif chunks[0] == 0:
                    dve.wait_ge(key_in, fetch * 16)
                for c in chunks:
                    ins = v.scalar_tensor_tensor(out=flat[:, c * P:(c + 1) * P], in0=flat[:, c * P:(c + 1) * P],
                                                 scalar=key_col[:, bass.ds(cols + c, 1)], in1=later[:],
                                                 op0=ALU.is_equal, op1=ALU.mult, accum_out=later_n[:, c:c + 1])
                if chunks[-1] == n - 1:
                    ins.then_inc(keys_used, 1)
                    dve.wait_ge(keys_used, fetch + 1)
                    v.scalar_tensor_tensor(out=value[:, 0:n], in0=later_n[:, 0:n], scalar=0.0,
                                           in1=evalue[:, bass.ds(cols, n)], op0=ALU.is_equal,
                                           op1=ALU.mult).then_inc(valued, 1)
                    dve.wait_ge(valued, fetch + 1)

            def hot(col, c):
                slot = col % 4 if isinstance(col, int) else (CPI0 + c) % 4
                wait(dve, hot_used, col - 3)
                v.tensor_scalar(src_hot[:, slot], nodes[:], cols_f[:, 0, bass.ds(col, 1)], None, ALU.is_equal)
                v.tensor_scalar(dst_hot[:, slot], nodes[:], cols_f[:, 1, bass.ds(col, 1)], value[:, c:c + 1],
                                ALU.is_equal, ALU.mult).then_inc(hot_made, 1)

            for ko in range(KO):
                dve.wait_ge(ln_hi, ko + 1)
                v.tensor_tensor(hT_lo[:, ko], bank[ko][:, 0:N], hT_hi[:, ko].bitcast(F32),
                                ALU.subtract).then_inc(ln_lo, 1)

            def low_of(out_ap, i, j, b):
                dve.wait_ge(proj_hi_made, i * 3 + j + 1)
                return v.scalar_tensor_tensor(out=out_ap[0], in0=bank[BANK_PROJ + j][:, 0:N], scalar=b,
                                              in1=out_ap[1].bitcast(F32), op0=ALU.add, op1=ALU.subtract)

            def low_q(i, j):
                at = bass.ds(i, 1)
                low_of((qkv_lo[j][:, at, :], qkv_hi[j][:, at, :]), i, j, bias[:, j, at]).then_inc(proj_lo_made, 1)

            def low_before(i, j):
                low_q(i - (1 if j == 0 else 0), (j + 2) % 3)

            def first_iteration():
                compare(0, range(CPI0), CPI0, 0)
                for c in range(CPI0):
                    hot(c, c)
                compare(CPI0, range(CPI // 2), CPI, 1)
                low_q(0, 0)
                dve.wait_ge(w_lo_made, 3)
                split_at(1, 0)
                low_q(0, 1)
                split_at(1, 1)
                compare(CPI0, range(CPI // 2, CPI), CPI, 1)

            def stage1(i, next_edges=True, group_ends=False):
                after = i * CPI + CPI0
                for j in range(3):
                    for c in SPLIT[j][:4]:
                        hot(i * CPI + (CPI0 - CPI + c), c)
                    low_before(i, j)
                    for c in SPLIT[j][4:]:
                        hot(i * CPI + (CPI0 - CPI + c), c)
                    split_at(i + (j + 2) // 3, (j + 2) % 3)
                    if group_ends and j == 2:
                        read_group_a()
                    if next_edges and j:
                        compare(after, range(CPI // 2 * (j - 1), CPI // 2 * j), CPI, i + 1)

            def read_group_a():
                dve.wait_ge(group_done, 1)
                for n in range(NT):
                    ins = v.tensor_scalar(expo[:, n], bank[BANK_MASK + n][:, 0:N].bitcast(I32), 23, None,
                                          ALU.logical_shift_right)
                ins.then_inc(group_read, 1)

            first_iteration()
            dve.wait_ge(const_in, 32)
            v.tensor_reduce(hs[:, 0:1], b1c[:], AX.X, ALU.max, apply_absolute_value=True).then_inc(b1_max, 1)
            with dve.Fori(1, 3) as i:
                stage1(i)
            for n in range(NT):
                ins = v.tensor_scalar(diag_hot[:, n], nodes[:], tile_row[:, n:n + 1],
                                      2.0 ** (EXP_BASE - 1 - 127), ALU.is_equal, ALU.mult)
            ins.then_inc(diag_made, 1)
            stage1(3, group_ends=True)
            dve.wait_ge(ew_exp, 1)
            step(v.tensor_scalar(ew_s[:, 3], ew[:], 0.0, None, ALU.max))
            step(v.tensor_tensor(ew_s[:, 4], ew_s[:, 3], ew_s[:, 2], ALU.add))
            step(v.tensor_scalar(ew_s[:, 3], ew_s[:, 4], 8.0, None, ALU.mult))
            with dve.Fori(4, KO - 2) as i:
                stage1(i)
            stage1(KO - 2, False)

            def last_edges():
                dve.wait_ge(group_done, 2)
                dve.wait_ge(group_read, 1)
                for n in range(NT):
                    ins = v.tensor_scalar(bits[n], bank[BANK_MASK + n][:, 0:N].bitcast(I32), 23, None,
                                          ALU.logical_shift_right)
                ins.then_inc(bits_read, 1)
                dve.wait_ge(bits_read, 1)
                for n in range(NT):
                    ins = v.scalar_tensor_tensor(out=m_f[n].bitcast(I32), in0=bits[n], scalar=0.0,
                                                 in1=expo[:, n], op0=ALU.is_equal, op1=ALU.mult)
                step(ins)
                for n in range(NT):
                    ins = v.tensor_tensor(expo[:, n], bits[n], m_f[n].bitcast(I32), ALU.add)
                step(ins)
                for n in range(NT):
                    v.tensor_scalar(bits[n], expo[:, n], ETYPES - 1, None, ALU.bitwise_and).then_inc(coded, 1)

            def hidden_scale():
                dve.wait_ge(b1_all, 1)
                step(v.tensor_scalar(hs[:, 2:3], hs[:, 1:2], H_SUM_MAX, None, ALU.add))
                step(v.tensor_scalar(hsi[:, 0:1], hs[:, 2:3].bitcast(I32), 23, None, ALU.logical_shift_right))
                step(v.tensor_scalar(hsi[:, 1:2], hsi[:, 0:1], -1.0, 268.0, ALU.mult, ALU.add))
                step(v.tensor_scalar(hsi[:, 2:3], hsi[:, 0:1], 14.0, None, ALU.subtract))
                step(v.tensor_scalar(hs[:, 3:4].bitcast(I32), hsi[:, 1:2], 23, None, ALU.logical_shift_left))
                step(v.tensor_scalar(hs[:, 5:6].bitcast(I32), hsi[:, 2:3], 23, None, ALU.logical_shift_left))
                step(v.tensor_scalar(hs[:, 4:5], hs[:, 3:4], 1.0 / H_SCALE, None, ALU.mult))
                step(v.tensor_scalar(b1s[:], b1c[:], hs[:, 3:4], None, ALU.mult))


            def make_mask(n):
                dve.wait_ge(coded, NT)
                step(v.tensor_scalar(mask8[:, n], expo[:, n], 0.0, NEG, ALU.is_equal, ALU.mult))
                for t in range(ETYPES):
                    step(v.tensor_scalar(m_f[n], bits[n], float(t), ew_s[:, 3, t:t + 1], ALU.is_equal,
                                         ALU.mult))
                    ins = v.tensor_tensor(mask8[:, n], mask8[:, n], m_f[n], ALU.add)
                    if t < ETYPES - 1:
                        step(ins)
                    else:
                        ins.then_inc(mask_made[n], 1)

            for j in range(3):
                low_before(KO - 1, j)
                split_at(KO - 1 + (j + 2) // 3, (j + 2) % 3)
                if j == 0:
                    last_edges()
            low_q(KO - 1, 2)
            make_mask(0)

            def stage2(i, project, attend):
                p = i - 1

                def mask_scores(k):
                    dve.wait_ge(scored, p * 6 + k + 1)
                    dve.sem_inc(scores_seen, 1)
                    dve.wait_ge(mask_made[k // 2], 1)
                    v.tensor_tensor_reduce(probs[:, k], bank[BANK_SCORE + k % 2][:, 0:N], mask8[:, k // 2],
                                           1.0, -3.4e38, ALU.add, ALU.max, sm[:, 0, k:k + 1]).then_inc(score_max, 1)
                    dve.wait_ge(score_max, p * 6 + k + 1)
                    v.tensor_scalar(sm[:, 1, k:k + 1], sm[:, 0, k:k + 1], -0.125, None, ALU.mult).then_inc(max_neg, 1)

                def norm(k):
                    dve.wait_ge(exped, p * 6 + k + 1)
                    v.reciprocal(sm[:, 3, k:k + 1], sm[:, 2, k:k + 1]).then_inc(inv_made, 1)
                    dve.wait_ge(inv_made, p * 6 + k + 1)
                    v.tensor_scalar(probs[:, k], probs[:, k], sm[:, 3, k:k + 1], None, ALU.mult).then_inc(normed, 1)

                def turn_v():
                    dve.wait_ge(turn_hi, p * 7 + 1)
                    v.tensor_tensor(v2_lo[:].rearrange("p a b -> p (a b)"), bank[BANK_TURN][:, 0:N],
                                    v2_hi[:].rearrange("p a b -> p (a b)").bitcast(F32),
                                    ALU.subtract).then_inc(turn_lo, 1)

                def turn(k):
                    n, h = k // 2, k % 2
                    at = slice(n * P, (n + 1) * P)
                    dve.wait_ge(turn_hi, p * 7 + k + 2)
                    v.tensor_tensor(pT_lo[h][:, :, at],
                                    bank[BANK_TURN + (k + 1) % 2][:, 0:N].rearrange("p (a b) -> p a b", a=NT),
                                    pT_hi[h][:, :, at].bitcast(F32), ALU.subtract).then_inc(turn_lo, 1)

                def pv_out(h):
                    rows = slice(HD * h, HD * h + HD)
                    dve.wait_ge(pv_hi, p * 2 + h + 1)
                    v.tensor_tensor(hT_lo[rows, bass.ds(p, 1), :], bank[BANK_PV][rows, 0:N],
                                    hT_hi[rows, bass.ds(p, 1), :].bitcast(F32), ALU.subtract).then_inc(pv_lo, 1)

                def project_out(j):
                    low_of(((q2_lo, k2_lo)[j][:], (q2_hi, k2_hi)[j][:]), i + KO, j,
                           bias[:, 3 + j, bass.ds(i, 1)]).then_inc(proj_lo_made, 1)

                def thresholds():
                    dve.wait_ge(gsum_all, 1)
                    step(v.tensor_scalar(gsum[:], bank[BANK_PV][:, 0:2], 1.0 / (F * D), None, ALU.mult))
                    v.tensor_scalar(thr[:], gsum[:], EPS, 0.5, ALU.add, ALU.mult).then_inc(gsum_all, 1)

                if attend:
                    mask_scores(0)
                    mask_scores(1)
                    if not project:
                        thresholds()
                    norm(0)
                    norm(1)
                    turn_v()
                    mask_scores(2)
                    mask_scores(3)
                    norm(2)
                    turn(0)
                    turn(1)
                    norm(3)
                    mask_scores(4)
                    mask_scores(5)
                    turn(2)
                    norm(4)
                    norm(5)
                    turn(3)
                if project:
                    project_out(0)
                if attend:
                    turn(4)
                split_at(i + KO, 2)
                if attend:
                    turn(5)
                if project:
                    project_out(1)
                if attend:
                    pv_out(0)
                if project:
                    split_at(i + KO + 1, 0)
                    split_at(i + KO + 1, 1)
                if attend:
                    pv_out(1)

            stage2(0, True, False)
            hidden_scale()
            with dve.Fori(1, PAIRS) as i:
                stage2(i, True, True)
            dve.wait_ge(gamma_done, FT)
            for m in range(2):
                ins = v.tensor_reduce(gsum[:, m:m + 1], gacc[:, m * FT // 2:(m + 1) * FT // 2], AX.X, ALU.add)
            ins.then_inc(gsum_made, 1)
            stage2(PAIRS, False, True)

            def ternary(t, u, m):
                dve.wait_ge(sgn_made, t * 2 + m + 1)
                if m == 0:
                    wait(dve, hid_done, t - 1)
                else:
                    wait(dve, y_step, t - 1)
                v.scalar_tensor_tensor(out=tern[:, m, u], in0=stream[:, 2 * m + u], scalar=thr[:, m:m + 1],
                                       in1=sgn[:, m, u], op0=ALU.is_gt, op1=ALU.min).then_inc(tern_made, 1)

            for s in range(stage3, SLABS):
                m = s - stage3
                if s + 3 < SLABS:
                    split_at(s // 3 + 1, s % 3)
                dve.wait_ge(o_turned, m + 1)
                if m in AHEAD:
                    k = m - AHEAD[0]
                    ternary(k // 2, k // 2, k % 2)
                at = slice(m * P, (m + 1) * P)
                v.tensor_tensor(xs[:, :, at], xs[:, :, at],
                                bank[BANK_TURN + m % 2][:, 0:N].rearrange("p (a b) -> p a b", a=NT),
                                ALU.add).then_inc(x_added, 1)
                dve.wait_ge(x_added, m + 1)
                for n in range(NT):
                    ins = v.bn_stats(stats[:, n, m], xs[:, n, at])
                if m == KO - 1:
                    step(ins)
            layer_norm(1, raw)
            for ko in range(KO):
                dve.wait_ge(ln_hi, KO + ko + 1)
                v.scalar_tensor_tensor(out=h2_lo[:, ko], in0=bank[ko][:, 0:N], scalar=H_SCALE, in1=h2_hi[:, ko],
                                       op0=ALU.mult, op1=ALU.subtract).then_inc(ln_lo, 1)

            def act_low(t, u):
                dve.wait_ge(act_hi_made, t + 1)
                v.tensor_tensor(act_lo[:, u], act[:, u], act_hi[:, u], ALU.subtract).then_inc(act_lo_made, 1)

            act_low(0, 0)
            ternary(1, 1, 1)
            with dve.Fori(1, FT // 2) as i:
                for u in range(2):
                    ternary(i * 2 + u, u, 0)
                    act_low(i * 2 + (u - 1), (u - 1) % 2)
                    ternary(i * 2 + u, u, 1)
            act_low(FT - 1, 1)
            dve.wait_ge(b2_added, NT)
            for k, (n, c) in enumerate(Y_PARTS):
                if (n, c) not in Y_BY_POOL:
                    dve.wait_ge(y_done, k + 1)
                    at = slice(c * 512, (c + 1) * 512)
                    v.scalar_tensor_tensor(out=xs[:, n, at], in0=bank[BANK_Y + 2 * n + c][:], scalar=hs[:, 5:6],
                                           in1=xs[:, n, at], op0=ALU.mult, op1=ALU.add).then_inc(y_ready[k], 1)

        @block.tensor
        def _(pe):
            t_ = nc.tensor

            pe.wait_ge(consts, 9)

            def turn_h(k, h):
                for half in range(2):
                    for n in range(NT):
                        pe.wait_ge(h_made, NT * (2 * k + half) + n + 1)
                        for ko in range(half * KO // 2, (half + 1) * KO // 2):
                            ins = t_.transpose(bank[ko][:, n * P:(n + 1) * P], h[:, n, ko * P:(ko + 1) * P], ident[:])
                            if n == NT - 1:
                                ins.then_inc(ln_turned, 1)

            turn_h(0, stream)

            def passes(outp, l_hi, l_lo, r_hi, r_lo, first, last):
                t_.matmul(outp, l_hi, r_hi, start=first, stop=False)
                t_.matmul(outp, l_hi, r_lo, start=False, stop=False)
                return t_.matmul(outp, l_lo, r_hi, start=False, stop=last)

            def project(s, j, r_hi, r_lo, kos):
                if kos[0] == 0:
                    pe.wait_ge(w_lo_made, s + 1)
                for ko in kos:
                    if isinstance(s, int) and s == 0:
                        pe.wait_ge(ln_lo, ko + 1)
                    w = slice(ko * P, (ko + 1) * P)
                    ins = passes(bank[BANK_PROJ + j][:, 0:N], w_hi[:, j, w], w_lo[:, j, w], r_hi[:, ko], r_lo[:, ko],
                                 ko == 0, ko == KO - 1)
                if kos[-1] == KO - 1:
                    ins.then_inc(slab_done, 1)

            def scatter(col, c, first=False):
                slot = col % 4 if isinstance(col, int) else (CPI0 + c) % 4
                pe.wait_ge(hot_made, col + 1)
                for n in range(NT):
                    ins = t_.matmul(bank[BANK_MASK + n][:, 0:N], src_hot[:, slot, n * P:(n + 1) * P],
                                    dst_hot[:, slot], start=first, stop=False)
                ins.then_inc(hot_used, 1)

            def flat_add(table, first, last):
                for n in range(NT):
                    ins = t_.matmul(bank[BANK_MASK + n][:, 0:N], ident_b[:], table(n), start=first, stop=last)
                return ins

            def project1(i, j):
                wait(pe, proj_lo_made, i * 3 + j - 2)
                project(i * 3 + j, j, hT_hi, hT_lo, range(KO))

            def stage1(i):
                for j in range(3):
                    project1(i, j)
                    for c in SPLIT[j]:
                        scatter(i * CPI + (CPI0 - CPI + c), c)

            for j in range(3):
                project1(0, j)
                if j == 1:
                    for c in range(CPI0):
                        scatter(c, c, c == 0)
            with pe.Fori(1, 4) as i:
                stage1(i)
            pe.wait_ge(diag_made, 1)
            flat_add(lambda n: diag_hot[:, n], False, True).then_inc(group_done, 1)
            pe.wait_ge(group_read, 1)
            flat_add(lambda n: zeros_b[:], True, False)
            with pe.Fori(4, KO - 1) as i:
                stage1(i)
            flat_add(lambda n: zeros_b[:], False, True).then_inc(group_done, 1)
            for j in range(3):
                project1(KO - 1, j)

            def stage2(i, do_project, attend):
                p = i - 1
                s = (i + KO) * 3

                def proj(j, part):
                    kos = ((0, 1, 2), (3, 4, 5), (6, 7))[part]
                    if do_project:
                        if part == 0 and j < 2:
                            pe.wait_ge(proj_lo_made, i * 2 + (3 * KO - 1 + j))
                        elif part == 0:
                            pe.wait_ge(proj_hi_made, s)
                        project(s + j, j, qkv_hi[j], qkv_lo[j], kos)
                    else:
                        if part == 0:
                            pe.wait_ge(pv_lo, 2 * PAIRS - 1)
                        project(s + j, j, hT_hi, hT_lo, [k for k in kos if k < PAIRS - 1])

                def score(n):
                    if not attend:
                        return
                    if n == 0:
                        pe.wait_ge(proj_lo_made, p * 2 + (3 * KO + 2))
                    else:
                        pe.wait_ge(score_max, p * 6 + 2 * n)
                    at = slice(n * P, (n + 1) * P)
                    for l, r, first, last in ((q2_hi, k2_hi, True, False), (q2_hi, k2_lo, False, False),
                                              (q2_lo, k2_hi, False, True)):
                        for h in range(2):
                            rows = slice(HD * h, HD * h + HD)
                            ins = t_.matmul(bank[BANK_SCORE + h][:, 0:N], l[rows, at], r[rows], start=first, stop=last)
                            if last:
                                ins.then_inc(scored, 1)

                def turn_v():
                    if not attend:
                        return
                    pe.wait_ge(proj_hi_made, s)
                    for n in range(NT):
                        at = slice(n * P, (n + 1) * P)
                        ins = t_.transpose(bank[BANK_TURN][:, at], v2T[:, at], ident[:])
                    ins.then_inc(turned_done, 1)

                def turn(k):
                    if not attend:
                        return
                    pe.wait_ge(normed, p * 6 + k + 1)
                    if k >= 1:
                        pe.wait_ge(turn_lo, p * 7 + k)
                    for n in range(NT):
                        ins = t_.transpose(bank[BANK_TURN + (k + 1) % 2][:, n * P:(n + 1) * P],
                                           probs[:, k, n * P:(n + 1) * P], ident[:])
                    ins.then_inc(turned_done, 1)

                def pv(h):
                    if not attend:
                        return
                    pe.wait_ge(turn_lo, p * 7 + 6 + h)
                    pe.wait_ge(pv_lo, p * 2 + h + 1)
                    for m in range(NT):
                        ins = passes(bank[BANK_PV][:, 0:N], v2_hi[:, m], v2_lo[:, m], pT_hi[h][:, m], pT_lo[h][:, m],
                                     m == 0, m == NT - 1)
                    ins.then_inc(pv_done, 1)

                if attend and not do_project:
                    pe.wait_ge(gsum_made, 1)
                    pe.wait_ge(pv_lo, 2 * PAIRS - 1)
                    t_.matmul(bank[BANK_PV][:, 0:2], ones[:], gsum[:], start=True, stop=True).then_inc(gsum_all, 1)
                score(0)
                proj(0, 0)
                turn_v()
                score(1)
                proj(0, 1)
                turn(0)
                turn(1)
                score(2)
                proj(0, 2)
                turn(2)
                proj(1, 0)
                turn(3)
                proj(1, 1)
                turn(4)
                proj(1, 2)
                turn(5)
                if attend and not do_project:
                    pe.wait_ge(gsum_all, 2)
                pv(0)
                proj(2, 0)
                pv(1)
                proj(2, 1)
                proj(2, 2)

            stage2(0, True, False)
            pe.wait_ge(bits_read, 1)
            with pe.Fori(1, PAIRS) as i:
                stage2(i, True, True)
            stage2(PAIRS, False, True)
            pe.wait_ge(pv_lo, 2 * PAIRS + 1)

            def turn_o(m):
                pe.wait_ge(o_biased, m + 1)
                wait(pe, x_added, m - 1)
                if m < 2:
                    pe.wait_ge(turn_lo, 7 * PAIRS)
                for n in range(NT):
                    at = slice(n * P, (n + 1) * P)
                    ins = t_.transpose(bank[BANK_TURN + m % 2][:, at], turned[:, at], ident[:])
                ins.then_inc(o_turned, 1)

            for s in range(stage3, SLABS):
                m = s - stage3
                j = s % 3
                wait(pe, o_biased, m - 2)
                project(s, j, hT_hi, hT_lo, range(KO) if m >= 3 else (KO - 1,))
                if m:
                    turn_o(m - 1)
            turn_o(KO - 1)

            turn_h(1, raw)

            def hidden(t, u):
                pe.wait_ge(tern_made, t * 2 + 1)
                wait(pe, relu_done, t - 1)
                for ko in range(KO):
                    if isinstance(t, int) and t == 0:
                        pe.wait_ge(ln_lo, KO + ko + 1)
                    for part, h in enumerate((h2_hi, h2_lo)):
                        ins = t_.matmul(bank[BANK_HID + u][:, 0:N], tern[:, 0, u, ko * P:(ko + 1) * P], h[:, ko],
                                        start=(ko == 0 and part == 0), stop=(ko == KO - 1 and part == 1))
                ins.then_inc(hid_done, 1)

            def output(t, u, tiles=range(NT), first=False, last=False):
                pe.wait_ge(tern_made, t * 2 + 2)
                pe.wait_ge(act_lo_made, t + 1)
                for n in tiles:
                    by_half = last and n == NT - 1
                    order = [(part, c) for c in range(2) for part in range(2)] if by_half else \
                            [(part, c) for part in range(2) for c in range(2)]
                    for part, c in order:
                        ins = t_.matmul(bank[BANK_Y + 2 * n + c][:], (act_hi, act_lo)[part][:, u, n * P:(n + 1) * P],
                                        tern[:, 1, u, c * 512:(c + 1) * 512],
                                        start=first and part == 0, stop=last and part == 1)
                        if last and part == 1:
                            ins.then_inc(y_done, 1)
                if not last and tiles[-1] == NT - 1:
                    ins.then_inc(y_step, 1)

            hidden(0, 0)
            hidden(1, 1)
            output(0, 0, first=True)
            with pe.Fori(1, FT // 2) as i:
                for u in range(2):
                    hidden(i * 2 + u, u)
                    if u == 0:
                        output(i * 2 - 1, 1)
                    else:
                        output(i * 2, 0)
            output(FT - 1, 1, last=True)


def kernel(x, src, dst, edge_type_5, L0_gnn_edge_type_weights, L0_gnn_wq, L0_gnn_bq, L0_gnn_wk, L0_gnn_bk,
           L0_gnn_wv, L0_gnn_bv, L0_gnn_wiq, L0_gnn_biq, L0_gnn_wik, L0_gnn_bik, L0_gnn_wiv, L0_gnn_biv,
           L0_gnn_wo, L0_gnn_bo, L0_ffn_W1, L0_ffn_b1, L0_ffn_W2, L0_ffn_b2):
    import numpy as np
    import concourse.bacc as bacc
    from concourse.bass_utils import run_bass_kernel_spmd

    def slabs(w):
        w = np.asarray(w)
        o, i = w.shape
        return w.reshape(o // P, P, i // P, P).transpose(0, 3, 2, 1).reshape(o // P, P, i)

    def turns(*ws):
        s = np.stack([slabs(w) for w in ws], axis=1)
        return s.reshape(-1, P, D)

    def columns(a):
        return np.ascontiguousarray(np.asarray(a).reshape(-1, P).T)

    w_slabs = np.concatenate([turns(L0_gnn_wq, L0_gnn_wk, L0_gnn_wv),
                              turns(L0_gnn_wiq, L0_gnn_wik, L0_gnn_wiv), slabs(L0_gnn_wo)])
    biases = np.stack([columns(b) for b in (L0_gnn_bq, L0_gnn_bk, L0_gnn_bv, L0_gnn_biq, L0_gnn_bik, L0_gnn_biv,
                                            L0_gnn_bo)], axis=1)
    ffn_slabs = np.concatenate([slabs(L0_ffn_W1), np.asarray(L0_ffn_W2).T.reshape(FT, P, D)])
    arrays = {
        "x": np.asarray(x),
        "edge_rows": np.stack([np.asarray(a).reshape(CH, P) for a in (src, dst)], axis=1),
        "edge_cols": np.stack([columns(a) for a in (src, dst, edge_type_5)], axis=1),
        "edge_w": np.asarray(L0_gnn_edge_type_weights),
        "w_slabs": w_slabs, "biases": biases, "ffn_slabs": ffn_slabs,
        "b1": columns(L0_ffn_b1), "b2": np.asarray(L0_ffn_b2),
    }
    arrays = {f"in_{k}": np.ascontiguousarray(v) for k, v in arrays.items()}
    nc = bacc.Bacc("TRN2", target_bir_lowering=False, num_devices=1)
    args = [nc.dram_tensor(k, v.shape, mybir.dt.from_np(v.dtype), kind="ExternalInput").ap() for k, v in arrays.items()]
    out = nc.dram_tensor("out", (N, D), F32, kind="ExternalOutput").ap()
    gnn_ffn_kernel(nc, *args, out)
    r = run_bass_kernel_spmd(nc, [arrays], core_ids=[0])
    return r.results[0]["out"]
```

```python
from contextlib import ExitStack

import concourse.bass as bass
from concourse import mybir

F32 = mybir.dt.float32
F32R = mybir.dt.float32r
BF16 = mybir.dt.bfloat16
F16 = mybir.dt.float16
I32 = mybir.dt.int32
ALU = mybir.AluOpType
ACT = mybir.ActivationFunctionType
AX = mybir.AxisListType

P = 128
N = 384
NT = N // P
D = 1024
KO = D // P
HD = 64
PAIRS = D // (2 * HD)
F = 4 * D
FT = F // P
E = 12672
CH = E // P
CPI = 16
CPI0 = 3
SPLIT = (range(0, 8), range(8, 12), range(12, 16))
COMPARED = (range(0, 5), range(5, 11), range(11, 16))
GROUP_A = CPI0 + 3 * CPI
ETYPES = 4
EPS = 1e-5
NEG = -3.0e38
EXP_BASE = 20
WO_BY_POOL = (3, 4, 6, 7)
H_SCALE = 1024.0
H_SUM_MAX = 1024.0

BANK_PROJ, BANK_SCORE, BANK_TURN, BANK_PV = 0, 3, 5, 7
BANK_MASK = 3
BANK_HID, BANK_Y = 0, 2
H_BANKS = ((6, 7), (0, 1), (6, 7))

Y_PARTS = [(n, c) for n in range(NT) for c in range(2)]
Y_BY_POOL = ((0, 1), (1, 1))
Y_ORDER = (0, 2, 1, 4, 3, 5)


def wait(eng, sem, value):
    if not (isinstance(value, int) and value <= 0):
        eng.wait_ge(sem, value)


def gnn_ffn_kernel(nc, x, edge_rows, edge_cols, edge_w, w_slabs, biases, bo, ffn_slabs, b1, b2, out):
    ctx = ExitStack()
    early, edges, pairs = ExitStack(), ExitStack(), ExitStack()
    late = ExitStack()
    with ctx:
        def sb(name, shape, dt, scope=ctx):
            return scope.enter_context(nc.sbuf_tensor(name, shape, dt))

        def sem(name):
            return ctx.enter_context(nc.semaphore(name))

        xs = sb("xs", [P, NT, D], F32)
        raw = sb("raw", [P, 3, D], F32)
        w_hi = sb("w_hi", [P, 3, D], F32R)
        w_lo = sb("w_lo", [P, 3, D], F32R)
        hT_hi = sb("hT_hi", [P, KO, N], F32R)
        hT_lo = sb("hT_lo", [P, KO, N], F32R)
        stream = sb("stream", [P, 4, D], F32)
        bias = sb("bias", [P, 6, KO], F32)
        b1c = sb("b1c", [P, FT], F32)
        b1s = sb("b1s", [P, FT], F32)
        ident = sb("ident", [P, P], F32)
        ones = sb("ones", [P, P], F32)
        stats = sb("stats", [P, NT, 2, 6], F32)
        mv = sb("mv", [P, NT, 2], F32)
        ln_s = sb("ln_s", [P, 6, NT], F32)
        gacc = sb("gacc", [P, FT], F32)
        gsum = sb("gsum", [P, 2], F32)
        thr = sb("thr", [P, 2], F32)
        hs = sb("hs", [P, 8], F32)
        hsi = sb("hsi", [P, 4], I32)
        qkv_hi = [sb(f"qkv_hi{j}", [P, KO, N], F32R, early) for j in range(3)]
        qkv_lo = [sb(f"qkv_lo{j}", [P, KO, N], F32R, early) for j in range(3)]
        mask8 = sb("mask8", [P, NT, N], F32, early)
        probs = sb("probs", [P, 6, N], F32, early)
        sm = sb("sm", [P, 4, 6], F32, early)
        ew = sb("ew", [P, ETYPES], F32, early)
        ew_s = sb("ew_s", [P, 5, ETYPES], F32, early)
        src_hot = sb("src_hot", [P, 4, N], BF16, edges)
        dst_hot = sb("dst_hot", [P, 4, N], BF16, edges)
        nodes = sb("nodes", [P, N], F16, edges)
        later = sb("later", [P, P], F32, edges)
        ident_b = sb("ident_b", [P, P], BF16, edges)
        diag_hot = sb("diag_hot", [P, NT, N], BF16, edges)
        zeros_b = sb("zeros_b", [P, N], BF16, edges)
        tile_row = sb("tile_row", [P, NT], F32, edges)
        rows_i = sb("rows_i", [CH, 2, P], I32, edges)
        key_rows = sb("key_rows", [CH, P], F32, edges)
        cols_i = sb("cols_i", [P, 3, CH], I32, edges)
        cols_f = sb("cols_f", [P, 2, CH], F32, edges)
        key_col = sb("key_col", [P, CH], F32, edges)
        expo = sb("expo", [P, NT, N], I32, edges)
        ebase = sb("ebase", [P, CH], I32, edges)
        etmp = sb("etmp", [P, 2, CH], I32, edges)
        later_n = sb("later_n", [P, CPI], F32, edges)
        value = sb("value", [P, CPI], F32, edges)
        edges.close()
        q2_hi = sb("q2_hi", [P, N], F32R, pairs)
        q2_lo = sb("q2_lo", [P, N], F32R, pairs)
        k2_hi = sb("k2_hi", [P, N], F32R, pairs)
        k2_lo = sb("k2_lo", [P, N], F32R, pairs)
        v2T = sb("v2T", [P, N], F32, pairs)
        v2_hi = sb("v2_hi", [P, NT, P], F32R, pairs)
        v2_lo = sb("v2_lo", [P, NT, P], F32R, pairs)
        pT_hi = [sb(f"pT_hi{h}", [P, NT, N], F32R, pairs) for h in range(2)]
        pT_lo = [sb(f"pT_lo{h}", [P, NT, N], F32R, pairs) for h in range(2)]
        pairs.close()
        early.close()
        wo_hi = sb("wo_hi", [P, KO - 3, D], F32R, late)
        wo_lo = sb("wo_lo", [P, KO - 3, D], F32R, late)
        bor = sb("bor", [P, D], F32, late)
        b2r = sb("b2r", [P, D], F32, late)
        sgn = sb("sgn", [P, 2, 2, D], F16, late)
        tern = sb("tern", [P, 2, 2, D], F16, late)
        h2_hi = sb("h2_hi", [P, KO, N], F16, late)
        h2_lo = sb("h2_lo", [P, KO, N], F16, late)
        act = sb("act", [P, 2, N], F32, late)
        act_hi = sb("act_hi", [P, 2, N], F16, late)
        act_lo = sb("act_lo", [P, 2, N], F16, late)
        late.close()
        bank = [ctx.enter_context(nc.psum_tensor(f"bank{i}", [P, 512], F32)) for i in range(8)]
        key_dram = nc.dram_tensor("key_scratch", [CH * P], F32, kind="Internal").ap()
        bits = [probs[:, 2 * n].bitcast(I32) for n in range(NT)]
        m_f = [probs[:, 2 * n + 1] for n in range(NT)]
        first_keys = mask8[:, 0]
        key_bc = probs[:, 0:6, :]

        x_in = [sem(f"x_in{n}") for n in range(NT)]
        ew_in = sem("ew_in")
        edges_in, const_in, rows_in = sem("edges_in"), sem("const_in"), sem("rows_in")
        raw_in = [sem(f"raw_in{j}") for j in range(3)]
        key_out, first_key_in, key_in = sem("key_out"), sem("first_key_in"), sem("key_in")
        gamma_in = [sem(f"gamma_in{u}") for u in range(2)]
        consts = sem("consts")
        key_made = sem("key_made")
        pre = sem("pre")
        a_pre = sem("a_pre")
        w_hi_made, w_lo_made, slab_done = sem("w_hi_made"), sem("w_lo_made"), sem("slab_done")
        wo_lo_made = [sem(f"wo_lo_made{k}") for k in range(3, KO)]
        proj_hi_made, proj_lo_made = sem("proj_hi_made"), sem("proj_lo_made")
        ln_turned, ln_hi, ln_lo = sem("ln_turned"), sem("ln_hi"), sem("ln_lo")
        var_made, sd_made = sem("var_made"), sem("sd_made")
        h_made = sem("h_made")
        gamma_done = sem("gamma_done")
        keys_used, valued = sem("keys_used"), sem("valued")
        hot_made, hot_used = sem("hot_made"), sem("hot_used")
        group_done, group_read = sem("group_done"), sem("group_read")
        ew_exp = sem("ew_exp")
        mask_made = [sem(f"mask_made{n}") for n in range(NT)]
        scored, score_max, max_neg, exped, inv_made, normed = (
            sem("scored"), sem("score_max"), sem("max_neg"), sem("exped"), sem("inv_made"), sem("normed"))
        turned_done, turn_hi, turn_lo = sem("turned_done"), sem("turn_hi"), sem("turn_lo")
        pv_done, pv_hi, pv_lo = sem("pv_done"), sem("pv_hi"), sem("pv_lo")
        gsum_made, gsum_all = sem("gsum_made"), sem("gsum_all")
        bo_in, bo_added, o_done, x_added = sem("bo_in"), sem("bo_added"), sem("o_done"), sem("x_added")
        scale_made = sem("scale_made")
        h2_made = [sem(f"h2_made{n}") for n in range(NT)]
        b1_max, b1_all = sem("b1_max"), sem("b1_all")
        ffn_in = [[sem(f"ffn_in{m}{u}") for u in range(2)] for m in range(2)]
        sgn_made, tern_made = sem("sgn_made"), sem("tern_made")
        hid_done, relu_done = sem("hid_done"), sem("relu_done")
        act_hi_made, act_lo_made = sem("act_hi_made"), sem("act_lo_made")
        y_step, y_done, y_scaled, out_done = sem("y_step"), sem("y_done"), sem("y_scaled"), sem("out_done")
        y_ready = [sem(f"y_ready{k}") for k in range(len(Y_PARTS))]
        b2_in = sem("b2_in")
        b2_added, diag_made = sem("b2_added"), sem("diag_made")
        scores_seen = sem("scores_seen")
        bits_read, coded = sem("bits_read"), sem("coded")
        p_pre, expo_read = sem("p_pre"), sem("expo_read")

        block = ctx.enter_context(nc.Block())
        stage3 = 2 * PAIRS * 3

        @block.sync
        def _(sp):
            sp.dma_start(ew[:], edge_w.partition_broadcast(P)).then_inc(ew_in, 16)
            for n in range(NT):
                sp.dma_start(xs[:, n], x[n * P:(n + 1) * P]).then_inc(x_in[n], 16)
            sp.dma_start(rows_i[:], edge_rows).then_inc(rows_in, 16)
            sp.dma_start(cols_i[:], edge_cols).then_inc(edges_in, 16)
            sp.dma_start(bias[:], biases).then_inc(const_in, 16)
            sp.wait_ge(key_made, 1)
            sp.dma_start(key_dram.rearrange("(c p) -> c p", p=P), key_rows[:]).then_inc(key_out, 16)
            sp.dma_start(raw[:, 0], w_slabs[0]).then_inc(raw_in[0], 16)
            sp.wait_ge(key_out, 16)
            sp.dma_start(first_keys[:, 0:CPI0 * P],
                         key_dram[0:CPI0 * P].partition_broadcast(P)).then_inc(first_key_in, 16)
            for j in range(1, 3):
                sp.dma_start(raw[:, j], w_slabs[j]).then_inc(raw_in[j], 16)
            flat_keys = key_bc.rearrange("p a b -> p (a b)")
            sp.dma_start(flat_keys[:, 0:CPI * P],
                         key_dram[CPI0 * P:(CPI0 + CPI) * P].partition_broadcast(P)).then_inc(key_in, 16)
            sp.dma_start(b1c[:], b1).then_inc(const_in, 16)

            def fetch_keys(b):
                sp.wait_ge(keys_used, b)
                sp.dma_start(flat_keys[:, 0:CPI * P],
                             key_dram[bass.ds(b * (CPI * P) + (CPI0 - CPI) * P, CPI * P)].partition_broadcast(P)
                             ).then_inc(key_in, 16)

            def fetch_slab(s, j):
                wait(sp, w_lo_made, s - 2)
                sp.dma_start(raw[:, j], w_slabs[s]).then_inc(raw_in[j], 16)

            def fetch_gamma(g, u):
                if isinstance(g, int) and g < 2:
                    sp.wait_ge(ln_turned, KO)
                else:
                    sp.wait_ge(gamma_done, g - 1)
                sp.dma_start(stream[:, 2 * u:2 * u + 2],
                             ffn_slabs[bass.ds(g * 2, 2)].rearrange("t p c -> p t c")).then_inc(gamma_in[u], 16)

            def iteration(i):
                fetch_gamma(i * 2, 0)
                fetch_slab(i * 3 + 3, 0)
                fetch_slab(i * 3 + 4, 1)
                fetch_gamma(i * 2 + 1, 1)
                fetch_slab(i * 3 + 5, 2)

            iteration(0)
            with sp.Fori(1, KO - 2) as i:
                fetch_keys(i + 1)
                iteration(i)
            with sp.Fori(KO - 2, KO + PAIRS) as i:
                iteration(i)
            fetch_slab(stage3 + 3, 0)
            fetch_slab(stage3 + 4, 1)
            sp.wait_ge(slab_done, stage3)
            sp.dma_start(bor[:], bo.partition_broadcast(P)).then_inc(bo_in, 16)
            fetch_slab(stage3 + 5, 2)
            for k in (6, 7):
                sp.wait_ge(wo_lo_made[k - 6], 1)
                sp.dma_start(raw[:, k % 3], w_slabs[stage3 + k]).then_inc(raw_in[k % 3], 16)
            sp.dma_start(b2r[:], b2.partition_broadcast(P)).then_inc(b2_in, 16)

            def fetch_ffn(t, u):
                for m in range(2):
                    if isinstance(t, int) and t < 2:
                        sp.wait_ge(gamma_done, FT)
                    else:
                        sp.wait_ge(tern_made, t * 2 + m - 3)
                    sp.dma_start(stream[:, 2 * m + u], ffn_slabs[t + m * FT]).then_inc(ffn_in[m][u], 16)

            for u in range(2):
                fetch_ffn(u, u)
            with sp.Fori(1, FT // 2) as i:
                for u in range(2):
                    fetch_ffn(i * 2 + u, u)
            for k in Y_ORDER:
                n, c = Y_PARTS[k]
                sp.wait_ge(y_ready[k], 1)
                sp.dma_start(out[n * P:(n + 1) * P, c * 512:(c + 1) * 512],
                             xs[:, n, c * 512:(c + 1) * 512]).then_inc(out_done, 16)
            sp.wait_ge(out_done, 16 * len(Y_PARTS))

        @block.gpsimd
        def _(pool):
            g = nc.gpsimd
            g.memset(ones[:], 1.0).then_inc(consts, 1)
            g.memset(zeros_b[:], 0.0).then_inc(consts, 1)
            pool.wait_ge(consts, 2)
            g.affine_select(out=ident[:], in_=ones[:], compare_op=ALU.is_equal, fill=0.0, base=0,
                            pattern=[[1, P]], channel_multiplier=-1).then_inc(consts, 1)
            g.affine_select(out=later[:], in_=ones[:], compare_op=ALU.is_gt, fill=0.0, base=0,
                            pattern=[[1, P]], channel_multiplier=-1).then_inc(consts, 1)
            g.iota(nodes[:], [[1, N]], base=0, channel_multiplier=0,
                   allow_small_or_imprecise_dtypes=True).then_inc(consts, 1)
            g.iota(tile_row[:], [[P, NT]], base=0, channel_multiplier=1,
                   allow_small_or_imprecise_dtypes=True).then_inc(consts, 1)
            g.iota(ebase[:, 0:GROUP_A], [[ETYPES, GROUP_A]], base=EXP_BASE, channel_multiplier=0).then_inc(consts, 1)
            g.iota(ebase[:, GROUP_A:CH], [[ETYPES, CH - GROUP_A]], base=EXP_BASE,
                   channel_multiplier=0).then_inc(consts, 1)
            pool.wait_ge(consts, 8)
            g.tensor_copy(ident_b[:], ident[:]).then_inc(consts, 1)

            for j in range(3):
                pool.wait_ge(w_hi_made, j + 1)
                g.tensor_tensor(w_lo[:, j], raw[:, j], w_hi[:, j].bitcast(F32), ALU.subtract).then_inc(w_lo_made, 1)

            pool.wait_ge(b1_max, 1)
            g.partition_all_reduce(hs[:, 1:2], hs[:, 0:1], P, bass.bass_isa.ReduceOp.max).then_inc(b1_all, 1)

            pcount = [0]

            def step(ins):
                pcount[0] += 1
                ins.then_inc(p_pre, 1)
                pool.wait_ge(p_pre, pcount[0])

            pool.wait_ge(coded, NT)
            n = NT - 1
            g.tensor_scalar(mask8[:, n], expo[:, n], 0.0, NEG, ALU.is_equal, ALU.mult).then_inc(expo_read, 1)
            pool.wait_ge(expo_read, 1)
            for t in range(ETYPES):
                step(g.tensor_scalar(m_f[n], bits[n], float(t), ew_s[:, 3, t:t + 1], ALU.is_equal, ALU.mult))
                ins = g.tensor_tensor(mask8[:, n], mask8[:, n], m_f[n], ALU.add)
                if t < ETYPES - 1:
                    step(ins)
                else:
                    ins.then_inc(mask_made[n], 1)

            for k in WO_BY_POOL:
                pool.wait_ge(w_hi_made, stage3 + k + 1)
                g.tensor_tensor(wo_lo[:, k - 3], raw[:, k % 3], wo_hi[:, k - 3].bitcast(F32),
                                ALU.subtract).then_inc(wo_lo_made[k - 3], 1)
            pool.wait_ge(bo_in, 16)
            pool.wait_ge(h_made, 2 * NT)
            for n in range(NT):
                g.tensor_tensor(xs[:, n], xs[:, n], bor[:], ALU.add).then_inc(bo_added, 1)
            pool.wait_ge(b2_in, 16)
            for n in range(NT):
                pool.wait_ge(h2_made[n], 2)
                g.tensor_tensor(xs[:, n], xs[:, n], b2r[:], ALU.add).then_inc(b2_added, 1)
            pool.wait_ge(b2_added, NT)
            for i, (n, c) in enumerate(Y_BY_POOL):
                at = slice(c * 512, (c + 1) * 512)
                pool.wait_ge(y_scaled, i + 1)
                g.tensor_tensor(xs[:, n, at], xs[:, n, at], raw[:, n, at],
                                ALU.add).then_inc(y_ready[Y_PARTS.index((n, c))], 1)

        @block.scalar
        def _(eng):
            a = nc.scalar
            count = [0]

            def step(ins):
                count[0] += 1
                ins.then_inc(a_pre, 1)
                eng.wait_ge(a_pre, count[0])

            eng.wait_ge(ew_in, 16)
            step(a.activation(ew_s[:, 0], ew[:], ACT.Abs))
            step(a.activation(ew_s[:, 1], ew_s[:, 0], ACT.Exp, scale=-1.0))
            step(a.activation(ew_s[:, 2], ew_s[:, 1], ACT.Ln, bias=1.0))
            step(a.activation(ew_s[:, 4], ew_s[:, 0], ACT.Sqrt))

            def root(k, tiles):
                eng.wait_ge(var_made, k + 1)
                a.activation(ln_s[:, 1, tiles], ln_s[:, 0, tiles], ACT.Sqrt, scale=0.25).then_inc(sd_made, 1)

            root(0, slice(0, NT))
            a.activation(ew_s[:, 4], ew_s[:, 0], ACT.Exp, scale=-1.0).then_inc(ew_exp, 1)

            def split_at(i, j):
                eng.wait_ge(raw_in[j], i * 16 + 16)
                wait(eng, slab_done, i * 3 + j - 2)
                a.activation(w_hi[:, j], raw[:, j], ACT.Copy).then_inc(w_hi_made, 1)

            split_at(0, 0)
            split_at(0, 1)
            for ko in range(KO):
                eng.wait_ge(ln_turned, ko + 1)
                a.activation(hT_hi[:, ko], bank[ko][:, 0:N], ACT.Copy).then_inc(ln_hi, 1)
            split_at(0, 2)

            def magnitudes(g, u):
                eng.wait_ge(gamma_in[u], (g // 2 + 1) * 16 if isinstance(g, int) else g * 8 + 16 - 8 * u)
                flat = stream[:, 2 * u:2 * u + 2].rearrange("p a b -> p (a b)")
                a.activation(flat, flat, ACT.Abs,
                             accum_out=gacc[:, bass.ds(g, 1)]).then_inc(gamma_done, 1)

            eng.wait_ge(const_in, 32)

            def stage1(i):
                for j in range(3):
                    if not isinstance(i, int) or j:
                        split_at(i + (j + 2) // 3, (j + 2) % 3)
                    if j == 0 or j == 1 and not isinstance(i, int):
                        magnitudes(i * 2 + j, j)
                    eng.wait_ge(slab_done, i * 3 + j + 1)
                    a.activation(qkv_hi[j][:, bass.ds(i, 1), :], bank[BANK_PROJ + j][:, 0:N], ACT.Identity,
                                 bias=bias[:, j, bass.ds(i, 1)]).then_inc(proj_hi_made, 1)

            stage1(0)
            magnitudes(1, 1)
            with eng.Fori(1, KO) as i:
                stage1(i)

            def stage2(i, project, attend):
                p = i - 1
                s = (i + KO) * 3

                def split_out(k):
                    eng.wait_ge(raw_in[k % 3], (2 * PAIRS + k // 3) * 16 + 16)
                    eng.wait_ge(slab_done, stage3)
                    a.activation(wo_hi[:, k - 3], raw[:, k % 3], ACT.Copy).then_inc(w_hi_made, 1)

                def exp(k):
                    eng.wait_ge(max_neg, p * 6 + k + 1)
                    a.activation(probs[:, k], probs[:, k], ACT.Exp, bias=sm[:, 1, k:k + 1], scale=0.125,
                                 accum_out=sm[:, 2, k:k + 1]).then_inc(exped, 1)

                def turn(k):
                    n, h = k // 2, k % 2
                    eng.wait_ge(turned_done, p * 7 + k + 2)
                    a.activation(pT_hi[h][:, :, n * P:(n + 1) * P],
                                 bank[BANK_TURN + (k + 1) % 2][:, 0:N].rearrange("p (a b) -> p a b", a=NT),
                                 ACT.Copy).then_inc(turn_hi, 1)

                def pv_out(h):
                    rows = slice(HD * h, HD * h + HD)
                    eng.wait_ge(pv_done, p * 2 + h + 1)
                    a.activation(hT_hi[rows, bass.ds(p, 1), :], bank[BANK_PV][rows, 0:N],
                                 ACT.Copy).then_inc(pv_hi, 1)

                def project_out(j):
                    eng.wait_ge(slab_done, s + j + 1)
                    if j < 2:
                        wait(eng, scored, p * 6 + 6)
                        a.activation((q2_hi, k2_hi)[j][:], bank[BANK_PROJ + j][:, 0:N], ACT.Identity,
                                     bias=bias[:, 3 + j, bass.ds(i, 1)]).then_inc(proj_hi_made, 1)
                    else:
                        a.activation(v2T[:], bank[BANK_PROJ + j][:, 0:N], ACT.Identity,
                                     bias=bias[:, 3 + j, bass.ds(i, 1)]).then_inc(proj_hi_made, 1)

                def turn_v():
                    eng.wait_ge(turned_done, p * 7 + 1)
                    a.activation(v2_hi[:].rearrange("p a b -> p (a b)"), bank[BANK_TURN][:, 0:N],
                                 ACT.Copy).then_inc(turn_hi, 1)

                if not project:
                    exp(0)
                    exp(1)
                    turn_v()
                    split_at(i + KO, 2)
                    exp(2)
                    exp(3)
                    split_out(3)
                    turn(0)
                    turn(1)
                    split_out(4)
                    turn(2)
                    exp(4)
                    exp(5)
                    split_out(5)
                    turn(3)
                    turn(4)
                    split_out(6)
                    turn(5)
                    split_out(7)
                    pv_out(0)
                    pv_out(1)
                    return
                if attend:
                    exp(0)
                    exp(1)
                    turn_v()
                    exp(2)
                    exp(3)
                    turn(0)
                    turn(1)
                split_at(i + KO, 2)
                if attend:
                    turn(2)
                    exp(4)
                project_out(0)
                if attend:
                    exp(5)
                    turn(3)
                    turn(4)
                if project:
                    project_out(1)
                if attend:
                    turn(5)
                if project:
                    split_at(i + KO + 1, 0)
                if attend:
                    pv_out(0)
                if project:
                    split_at(i + KO + 1, 1)
                    magnitudes((i + KO) * 2, 0)
                if attend:
                    pv_out(1)
                if project:
                    magnitudes((i + KO) * 2 + 1, 1)
                    project_out(2)

            stage2(0, True, False)
            eng.wait_ge(expo_read, 1)
            with eng.Fori(1, PAIRS) as i:
                stage2(i, True, True)
            stage2(PAIRS, False, True)

            def signs(t, u, m):
                eng.wait_ge(ffn_in[m][u], (t // 2 + 1) * 16 if isinstance(t, int) else t * 8 + 16 - 8 * u)
                wait(eng, tern_made, t * 2 + m - 3)
                a.activation(sgn[:, m, u], stream[:, 2 * m + u], ACT.Sign, bias=thr[:, m:m + 1]).then_inc(sgn_made, 1)

            def ln_high(n):
                for half in range(2):
                    eng.wait_ge(ln_turned, KO + 2 * n + half + 1)
                    a.activation(h2_hi[:, half * 4:half * 4 + 4, n * P:(n + 1) * P],
                                 bank[H_BANKS[n][half]][:].rearrange("p (a b) -> p a b", a=4), ACT.Copy,
                                 scale=H_SCALE).then_inc(ln_hi, 1)

            eng.wait_ge(gsum_all, 2)
            signs(0, 0, 0)
            signs(0, 0, 1)
            signs(1, 1, 0)
            root(1, slice(0, 2))
            ln_high(0)
            ln_high(1)
            root(2, slice(2, 3))
            ln_high(2)
            signs(1, 1, 1)

            def relu(t, u):
                eng.wait_ge(hid_done, t + 1)
                wait(eng, act_lo_made, t - 1)
                a.activation(act[:, u], bank[BANK_HID + u][:, 0:N], ACT.Relu, bias=b1s[:, bass.ds(t, 1)],
                             scale=hs[:, 4:5]).then_inc(relu_done, 1)
                eng.wait_ge(relu_done, t + 1)
                wait(eng, y_step, t - 1)
                a.activation(act_hi[:, u], act[:, u], ACT.Copy).then_inc(act_hi_made, 1)

            relu(0, 0)
            with eng.Fori(1, FT // 2) as i:
                for u in range(2):
                    signs(i * 2 + u, u, 0)
                    relu(i * 2 + (u - 1), (u - 1) % 2)
                    signs(i * 2 + u, u, 1)
            relu(FT - 1, 1)
            for k, (n, c) in enumerate(Y_PARTS):
                if (n, c) in Y_BY_POOL:
                    eng.wait_ge(y_done, k + 1)
                    a.activation(raw[:, n, c * 512:(c + 1) * 512], bank[BANK_Y + 2 * n + c][:], ACT.Copy,
                                 scale=hs[:, 5:6]).then_inc(y_scaled, 1)

        @block.vector
        def _(dve):
            v = nc.vector
            count = [0]

            def step(ins):
                count[0] += 1
                ins.then_inc(pre, 1)
                dve.wait_ge(pre, count[0])

            dve.sem_inc(pv_lo, 1)
            evalue = etmp[:, 1].bitcast(F32)

            def row_keys():
                dve.wait_ge(rows_in, 16)
                v.scalar_tensor_tensor(out=key_rows[:], in0=rows_i[:, 0], scalar=float(N), in1=rows_i[:, 1],
                                       op0=ALU.mult, op1=ALU.add).then_inc(key_made, 1)

            def edge_values():
                dve.wait_ge(consts, 9)
                dve.wait_ge(edges_in, 16)
                v.tensor_copy(cols_f[:], cols_i[:, 0:2])
                step(v.scalar_tensor_tensor(out=key_col[:], in0=cols_i[:, 0], scalar=float(N), in1=cols_i[:, 1],
                                            op0=ALU.mult, op1=ALU.add))
                step(v.tensor_scalar(etmp[:, 0], cols_i[:, 2], float(ETYPES - 1), None, ALU.add))
                step(v.tensor_scalar(etmp[:, 1], etmp[:, 0], ETYPES - 1, None, ALU.bitwise_and))
                step(v.tensor_tensor(etmp[:, 0], etmp[:, 1], ebase[:], ALU.add))
                step(v.tensor_scalar(etmp[:, 1], etmp[:, 0], 23, None, ALU.logical_shift_left))

            def scales(k, tiles):
                v.tensor_scalar(ln_s[:, 0, tiles], mv[:, tiles, 1], EPS, None, ALU.add).then_inc(var_made, 1)
                dve.wait_ge(sd_made, k + 1)
                step(v.reciprocal(ln_s[:, 2, tiles], ln_s[:, 1, tiles]))
                step(v.tensor_tensor(ln_s[:, 3, tiles], ln_s[:, 2, tiles], ln_s[:, 0, tiles], ALU.mult))
                step(v.scalar_tensor_tensor(out=ln_s[:, 4, tiles], in0=ln_s[:, 3, tiles], scalar=0.25,
                                            in1=ln_s[:, 1, tiles], op0=ALU.mult, op1=ALU.add))
                v.reciprocal(ln_s[:, 5, tiles], ln_s[:, 4, tiles]).then_inc(scale_made, 1)
                dve.wait_ge(scale_made, k + 1)

            def normalized(h, n, half, made):
                at = slice(half * D // 2, (half + 1) * D // 2)
                v.tensor_scalar(h[:, n, at], xs[:, n, at], mv[:, n, 0:1], ln_s[:, 5, n:n + 1], ALU.subtract,
                                ALU.mult).then_inc(made, 1)

            for n in range(NT):
                if n == NT - 1:
                    row_keys()
                dve.wait_ge(x_in[n], 16)
                for c in range(2):
                    step(v.bn_stats(stats[:, n, c], xs[:, n, c * 512:(c + 1) * 512]))
                ins = v.bn_aggr(mv[:, n], stats[:, n])
            step(ins)
            scales(0, slice(0, NT))
            for half in range(2):
                for n in range(NT):
                    normalized(stream, n, half, h_made)
            edge_values()

            def split_at(i, j):
                dve.wait_ge(w_hi_made, i * 3 + j + 1)
                v.tensor_tensor(w_lo[:, j], raw[:, j], w_hi[:, j].bitcast(F32), ALU.subtract).then_inc(w_lo_made, 1)

            def compare(cols, chunks, n, fetch):
                flat = key_bc.rearrange("p a b -> p (a b)") if n == CPI else first_keys
                if n == CPI0:
                    dve.wait_ge(first_key_in, 16)
                elif chunks[0] == 0:
                    dve.wait_ge(key_in, fetch * 16)
                for c in chunks:
                    ins = v.scalar_tensor_tensor(out=flat[:, c * P:(c + 1) * P], in0=flat[:, c * P:(c + 1) * P],
                                                 scalar=key_col[:, bass.ds(cols + c, 1)], in1=later[:],
                                                 op0=ALU.is_equal, op1=ALU.mult, accum_out=later_n[:, c:c + 1])
                if chunks[-1] == n - 1:
                    ins.then_inc(keys_used, 1)
                    dve.wait_ge(keys_used, fetch + 1)
                    v.scalar_tensor_tensor(out=value[:, 0:n], in0=later_n[:, 0:n], scalar=0.0,
                                           in1=evalue[:, bass.ds(cols, n)], op0=ALU.is_equal,
                                           op1=ALU.mult).then_inc(valued, 1)
                    dve.wait_ge(valued, fetch + 1)

            def hot(col, c):
                slot = col % 4 if isinstance(col, int) else (CPI0 + c) % 4
                wait(dve, hot_used, col - 3)
                v.tensor_scalar(src_hot[:, slot], nodes[:], cols_f[:, 0, bass.ds(col, 1)], None, ALU.is_equal)
                v.tensor_scalar(dst_hot[:, slot], nodes[:], cols_f[:, 1, bass.ds(col, 1)], value[:, c:c + 1],
                                ALU.is_equal, ALU.mult).then_inc(hot_made, 1)

            for ko in range(KO):
                dve.wait_ge(ln_hi, ko + 1)
                v.tensor_tensor(hT_lo[:, ko], bank[ko][:, 0:N], hT_hi[:, ko].bitcast(F32),
                                ALU.subtract).then_inc(ln_lo, 1)

            def low_of(out_ap, i, j, b):
                dve.wait_ge(proj_hi_made, i * 3 + j + 1)
                return v.scalar_tensor_tensor(out=out_ap[0], in0=bank[BANK_PROJ + j][:, 0:N], scalar=b,
                                              in1=out_ap[1].bitcast(F32), op0=ALU.add, op1=ALU.subtract)

            def low_q(i, j):
                at = bass.ds(i, 1)
                low_of((qkv_lo[j][:, at, :], qkv_hi[j][:, at, :]), i, j, bias[:, j, at]).then_inc(proj_lo_made, 1)

            def diagonal():
                for n in range(NT):
                    ins = v.tensor_scalar(diag_hot[:, n], nodes[:], tile_row[:, n:n + 1],
                                          2.0 ** (EXP_BASE - 1 - 127), ALU.is_equal, ALU.mult)
                ins.then_inc(diag_made, 1)

            def low_before(i, j):
                low_q(i - (1 if j == 0 else 0), (j + 2) % 3)

            def first_iteration():
                compare(0, range(CPI0), CPI0, 0)
                for c in range(CPI0):
                    hot(c, c)
                compare(CPI0, range(CPI // 2), CPI, 1)
                low_q(0, 0)
                dve.wait_ge(w_lo_made, 3)
                split_at(1, 0)
                low_q(0, 1)
                split_at(1, 1)
                compare(CPI0, range(CPI // 2, CPI), CPI, 1)

            def stage1(i, next_edges=True, group_ends=False):
                after = i * CPI + CPI0
                for j in range(3):
                    for c in SPLIT[j]:
                        hot(i * CPI + (CPI0 - CPI + c), c)
                    low_before(i, j)
                    split_at(i + (j + 2) // 3, (j + 2) % 3)
                    if group_ends and j == 1:
                        diagonal()
                    if group_ends and j == 2:
                        read_group_a()
                    if next_edges:
                        compare(after, COMPARED[j], CPI, i + 1)

            def read_group_a():
                dve.wait_ge(group_done, 1)
                for n in range(NT):
                    ins = v.tensor_scalar(expo[:, n], bank[BANK_MASK + n][:, 0:N].bitcast(I32), 23, None,
                                          ALU.logical_shift_right)
                ins.then_inc(group_read, 1)

            first_iteration()
            dve.wait_ge(const_in, 32)
            v.tensor_reduce(hs[:, 0:1], b1c[:], AX.X, ALU.max, apply_absolute_value=True).then_inc(b1_max, 1)
            with dve.Fori(1, 3) as i:
                stage1(i)
            stage1(3, group_ends=True)
            dve.wait_ge(ew_exp, 1)
            step(v.tensor_scalar(ew_s[:, 3], ew[:], 0.0, None, ALU.max))
            step(v.tensor_tensor(ew_s[:, 4], ew_s[:, 3], ew_s[:, 2], ALU.add))
            step(v.tensor_scalar(ew_s[:, 3], ew_s[:, 4], 8.0, None, ALU.mult))
            with dve.Fori(4, KO - 2) as i:
                stage1(i)
            stage1(KO - 2, False)

            def last_edges():
                dve.wait_ge(group_done, 2)
                dve.wait_ge(group_read, 1)
                for n in range(NT):
                    ins = v.tensor_scalar(bits[n], bank[BANK_MASK + n][:, 0:N].bitcast(I32), 23, None,
                                          ALU.logical_shift_right)
                ins.then_inc(bits_read, 1)
                dve.wait_ge(bits_read, 1)
                for n in range(NT):
                    ins = v.scalar_tensor_tensor(out=m_f[n].bitcast(I32), in0=bits[n], scalar=0.0,
                                                 in1=expo[:, n], op0=ALU.is_equal, op1=ALU.mult)
                step(ins)
                for n in range(NT):
                    ins = v.tensor_tensor(expo[:, n], bits[n], m_f[n].bitcast(I32), ALU.add)
                step(ins)
                for n in range(NT):
                    v.tensor_scalar(bits[n], expo[:, n], ETYPES - 1, None, ALU.bitwise_and).then_inc(coded, 1)

            def hidden_scale():
                dve.wait_ge(b1_all, 1)
                step(v.tensor_scalar(hs[:, 2:3], hs[:, 1:2], H_SUM_MAX, None, ALU.add))
                step(v.tensor_scalar(hsi[:, 0:1], hs[:, 2:3].bitcast(I32), 23, None, ALU.logical_shift_right))
                step(v.tensor_scalar(hsi[:, 1:2], hsi[:, 0:1], -1.0, 268.0, ALU.mult, ALU.add))
                step(v.tensor_scalar(hsi[:, 2:3], hsi[:, 0:1], 14.0, None, ALU.subtract))
                step(v.tensor_scalar(hs[:, 3:4].bitcast(I32), hsi[:, 1:2], 23, None, ALU.logical_shift_left))
                step(v.tensor_scalar(hs[:, 5:6].bitcast(I32), hsi[:, 2:3], 23, None, ALU.logical_shift_left))
                step(v.tensor_scalar(hs[:, 4:5], hs[:, 3:4], 1.0 / H_SCALE, None, ALU.mult))
                step(v.tensor_scalar(b1s[:], b1c[:], hs[:, 3:4], None, ALU.mult))


            def make_mask(n, weights=range(ETYPES)):
                dve.wait_ge(coded, NT)
                if weights[0] == 0:
                    step(v.tensor_scalar(mask8[:, n], expo[:, n], 0.0, NEG, ALU.is_equal, ALU.mult))
                for t in weights:
                    step(v.tensor_scalar(m_f[n], bits[n], float(t), ew_s[:, 3, t:t + 1], ALU.is_equal,
                                         ALU.mult))
                    ins = v.tensor_tensor(mask8[:, n], mask8[:, n], m_f[n], ALU.add)
                    if t < ETYPES - 1:
                        step(ins)
                    else:
                        ins.then_inc(mask_made[n], 1)

            for j in range(3):
                low_before(KO - 1, j)
                split_at(KO - 1 + (j + 2) // 3, (j + 2) % 3)
                if j == 0:
                    last_edges()
                else:
                    make_mask(0, range(ETYPES)[2 * j - 2:2 * j])
            low_q(KO - 1, 2)
            make_mask(1, range(2))

            def stage2(i, project, attend):
                p = i - 1

                def mask_scores(k):
                    dve.wait_ge(scored, p * 6 + k + 1)
                    dve.sem_inc(scores_seen, 1)
                    dve.wait_ge(mask_made[k // 2], 1)
                    v.tensor_tensor_reduce(probs[:, k], bank[BANK_SCORE + k % 2][:, 0:N], mask8[:, k // 2],
                                           1.0, -3.4e38, ALU.add, ALU.max, sm[:, 0, k:k + 1]).then_inc(score_max, 1)
                    dve.wait_ge(score_max, p * 6 + k + 1)
                    v.tensor_scalar(sm[:, 1, k:k + 1], sm[:, 0, k:k + 1], -0.125, None, ALU.mult).then_inc(max_neg, 1)

                def norm(k):
                    dve.wait_ge(exped, p * 6 + k + 1)
                    v.reciprocal(sm[:, 3, k:k + 1], sm[:, 2, k:k + 1]).then_inc(inv_made, 1)
                    dve.wait_ge(inv_made, p * 6 + k + 1)
                    v.tensor_scalar(probs[:, k], probs[:, k], sm[:, 3, k:k + 1], None, ALU.mult).then_inc(normed, 1)

                def turn_v():
                    dve.wait_ge(turn_hi, p * 7 + 1)
                    v.tensor_tensor(v2_lo[:].rearrange("p a b -> p (a b)"), bank[BANK_TURN][:, 0:N],
                                    v2_hi[:].rearrange("p a b -> p (a b)").bitcast(F32),
                                    ALU.subtract).then_inc(turn_lo, 1)

                def turn(k):
                    n, h = k // 2, k % 2
                    at = slice(n * P, (n + 1) * P)
                    dve.wait_ge(turn_hi, p * 7 + k + 2)
                    v.tensor_tensor(pT_lo[h][:, :, at],
                                    bank[BANK_TURN + (k + 1) % 2][:, 0:N].rearrange("p (a b) -> p a b", a=NT),
                                    pT_hi[h][:, :, at].bitcast(F32), ALU.subtract).then_inc(turn_lo, 1)

                def pv_out(h):
                    rows = slice(HD * h, HD * h + HD)
                    dve.wait_ge(pv_hi, p * 2 + h + 1)
                    v.tensor_tensor(hT_lo[rows, bass.ds(p, 1), :], bank[BANK_PV][rows, 0:N],
                                    hT_hi[rows, bass.ds(p, 1), :].bitcast(F32), ALU.subtract).then_inc(pv_lo, 1)

                def project_out(j):
                    low_of(((q2_lo, k2_lo)[j][:], (q2_hi, k2_hi)[j][:]), i + KO, j,
                           bias[:, 3 + j, bass.ds(i, 1)]).then_inc(proj_lo_made, 1)

                def sum_magnitudes():
                    dve.wait_ge(gamma_done, FT)
                    for m in range(2):
                        ins = v.tensor_reduce(gsum[:, m:m + 1], gacc[:, m * FT // 2:(m + 1) * FT // 2], AX.X, ALU.add)
                    ins.then_inc(gsum_made, 1)

                def thresholds():
                    dve.wait_ge(gsum_all, 1)
                    step(v.tensor_scalar(gsum[:], bank[BANK_PV][:, 0:2], 1.0 / (F * D), None, ALU.mult))
                    v.tensor_scalar(thr[:], gsum[:], EPS, 0.5, ALU.add, ALU.mult).then_inc(gsum_all, 1)

                if not project:
                    mask_scores(0)
                    mask_scores(1)
                    norm(0)
                    norm(1)
                    sum_magnitudes()
                    turn_v()
                    mask_scores(2)
                    mask_scores(3)
                    norm(2)
                    split_at(i + KO, 2)
                    turn(0)
                    turn(1)
                    norm(3)
                    mask_scores(4)
                    mask_scores(5)
                    turn(2)
                    norm(4)
                    norm(5)
                    turn(3)
                    dve.wait_ge(w_hi_made, stage3 + 6)
                    v.tensor_tensor(wo_lo[:, 2], raw[:, 2], wo_hi[:, 2].bitcast(F32),
                                    ALU.subtract).then_inc(wo_lo_made[2], 1)
                    thresholds()
                    turn(4)
                    turn(5)
                    pv_out(0)
                    pv_out(1)
                    return
                if attend:
                    mask_scores(0)
                    mask_scores(1)
                    norm(0)
                    norm(1)
                    turn_v()
                    mask_scores(2)
                    mask_scores(3)
                    norm(2)
                    turn(0)
                    turn(1)
                    norm(3)
                    mask_scores(4)
                    mask_scores(5)
                    turn(2)
                    norm(4)
                    norm(5)
                    turn(3)
                if project:
                    project_out(0)
                if attend:
                    turn(4)
                split_at(i + KO, 2)
                if attend:
                    turn(5)
                if project:
                    project_out(1)
                if attend:
                    pv_out(0)
                if project:
                    split_at(i + KO + 1, 0)
                    split_at(i + KO + 1, 1)
                if attend:
                    pv_out(1)

            stage2(0, True, False)
            make_mask(1, range(2, ETYPES))
            with dve.Fori(1, PAIRS) as i:
                stage2(i, True, True)
            stage2(PAIRS, False, True)
            hidden_scale()

            def ternary(t, u, m):
                dve.wait_ge(sgn_made, t * 2 + m + 1)
                if m == 0:
                    wait(dve, hid_done, t - 1)
                else:
                    wait(dve, y_step, t - 1)
                v.scalar_tensor_tensor(out=tern[:, m, u], in0=stream[:, 2 * m + u], scalar=thr[:, m:m + 1],
                                       in1=sgn[:, m, u], op0=ALU.is_gt, op1=ALU.min).then_inc(tern_made, 1)

            def residual(k):
                n, c = Y_PARTS[k]
                at = slice(c * 512, (c + 1) * 512)
                dve.wait_ge(bo_added, n + 1)
                dve.wait_ge(o_done, k + 1)
                v.tensor_tensor(xs[:, n, at], xs[:, n, at], bank[k][:], ALU.add).then_inc(x_added, 1)

            def statistics(k):
                n, c = Y_PARTS[k]
                dve.wait_ge(x_added, k + 1)
                return v.bn_stats(stats[:, n, c], xs[:, n, c * 512:(c + 1) * 512])

            def ln_low(n):
                for half in range(2):
                    at = (slice(None), slice(half * 4, half * 4 + 4), slice(n * P, (n + 1) * P))
                    dve.wait_ge(ln_hi, KO + 2 * n + half + 1)
                    v.scalar_tensor_tensor(out=h2_lo[at], in0=bank[H_BANKS[n][half]][:].rearrange(
                        "p (a b) -> p a b", a=4), scalar=H_SCALE, in1=h2_hi[at],
                        op0=ALU.mult, op1=ALU.subtract).then_inc(ln_lo, 1)

            ternary(0, 0, 0)
            ternary(0, 0, 1)
            ternary(1, 1, 0)
            for n in range(2):
                residual(2 * n)
                residual(2 * n + 1)
                statistics(2 * n)
                step(statistics(2 * n + 1))
                ins = v.bn_aggr(mv[:, n], stats[:, n])
            step(ins)
            scales(1, slice(0, 2))
            for n in range(2):
                for half in range(2):
                    normalized(raw, n, half, h2_made[n])
            residual(4)
            statistics(4)
            ln_low(0)
            ln_low(1)
            residual(5)
            step(statistics(5))
            step(v.bn_aggr(mv[:, 2], stats[:, 2]))
            scales(2, slice(2, 3))
            for half in range(2):
                normalized(raw, 2, half, h2_made[2])
            ln_low(2)

            def act_low(t, u):
                dve.wait_ge(act_hi_made, t + 1)
                v.tensor_tensor(act_lo[:, u], act[:, u], act_hi[:, u], ALU.subtract).then_inc(act_lo_made, 1)

            act_low(0, 0)
            ternary(1, 1, 1)
            with dve.Fori(1, FT // 2) as i:
                for u in range(2):
                    ternary(i * 2 + u, u, 0)
                    act_low(i * 2 + (u - 1), (u - 1) % 2)
                    ternary(i * 2 + u, u, 1)
            act_low(FT - 1, 1)
            dve.wait_ge(b2_added, NT)
            for k, (n, c) in enumerate(Y_PARTS):
                if (n, c) not in Y_BY_POOL:
                    dve.wait_ge(y_done, k + 1)
                    at = slice(c * 512, (c + 1) * 512)
                    v.scalar_tensor_tensor(out=xs[:, n, at], in0=bank[BANK_Y + 2 * n + c][:], scalar=hs[:, 5:6],
                                           in1=xs[:, n, at], op0=ALU.mult, op1=ALU.add).then_inc(y_ready[k], 1)

        @block.tensor
        def _(pe):
            t_ = nc.tensor

            pe.wait_ge(consts, 9)

            for half in range(2):
                for n in range(NT):
                    pe.wait_ge(h_made, NT * half + n + 1)
                    for ko in range(half * KO // 2, (half + 1) * KO // 2):
                        ins = t_.transpose(bank[ko][:, n * P:(n + 1) * P], stream[:, n, ko * P:(ko + 1) * P], ident[:])
                        if n == NT - 1:
                            ins.then_inc(ln_turned, 1)

            def passes(outp, l_hi, l_lo, r_hi, r_lo, first, last):
                t_.matmul(outp, l_hi, r_hi, start=first, stop=False)
                t_.matmul(outp, l_hi, r_lo, start=False, stop=False)
                return t_.matmul(outp, l_lo, r_hi, start=False, stop=last)

            def project(s, j, r_hi, r_lo, kos):
                if kos[0] == 0:
                    pe.wait_ge(w_lo_made, s + 1)
                for ko in kos:
                    if isinstance(s, int) and s == 0:
                        pe.wait_ge(ln_lo, ko + 1)
                    w = slice(ko * P, (ko + 1) * P)
                    ins = passes(bank[BANK_PROJ + j][:, 0:N], w_hi[:, j, w], w_lo[:, j, w], r_hi[:, ko], r_lo[:, ko],
                                 ko == 0, ko == KO - 1)
                if kos[-1] == KO - 1:
                    ins.then_inc(slab_done, 1)

            def scatter(col, c, first=False):
                slot = col % 4 if isinstance(col, int) else (CPI0 + c) % 4
                pe.wait_ge(hot_made, col + 1)
                for n in range(NT):
                    ins = t_.matmul(bank[BANK_MASK + n][:, 0:N], src_hot[:, slot, n * P:(n + 1) * P],
                                    dst_hot[:, slot], start=first, stop=False)
                ins.then_inc(hot_used, 1)

            def flat_add(table, first, last):
                for n in range(NT):
                    ins = t_.matmul(bank[BANK_MASK + n][:, 0:N], ident_b[:], table(n), start=first, stop=last)
                return ins

            def project1(i, j):
                wait(pe, proj_lo_made, i * 3 + j - 2)
                project(i * 3 + j, j, hT_hi, hT_lo, range(KO))

            def stage1(i, begun=False):
                for j in range(3):
                    if j or not begun:
                        project1(i, j)
                    for c in SPLIT[j]:
                        scatter(i * CPI + (CPI0 - CPI + c), c)

            for j in range(3):
                project1(0, j)
                if j == 1:
                    for c in range(CPI0):
                        scatter(c, c, c == 0)
            with pe.Fori(1, 4) as i:
                stage1(i)
            pe.wait_ge(diag_made, 1)
            flat_add(lambda n: diag_hot[:, n], False, True).then_inc(group_done, 1)
            project1(4, 0)
            pe.wait_ge(group_read, 1)
            flat_add(lambda n: zeros_b[:], True, False)
            stage1(4, begun=True)
            with pe.Fori(5, KO - 1) as i:
                stage1(i)
            flat_add(lambda n: zeros_b[:], False, True).then_inc(group_done, 1)
            for j in range(3):
                project1(KO - 1, j)

            def out_part(y, kos):
                n, c = Y_PARTS[y]
                if kos[0] == 0:
                    if y == 0:
                        pe.wait_ge(pv_lo, 2 * PAIRS - 1)
                    elif y == 2:
                        pe.wait_ge(proj_hi_made, stage3)
                    elif y == 3:
                        pe.wait_ge(score_max, 6 * PAIRS)
                    elif y == 5:
                        pe.wait_ge(turn_lo, 7 * PAIRS)
                for ko in kos:
                    if ko < 3:
                        pe.wait_ge(w_lo_made, stage3 + ko + 1)
                    else:
                        pe.wait_ge(wo_lo_made[ko - 3], 1)
                    hi, lo = (w_hi[:, ko], w_lo[:, ko]) if ko < 3 else (wo_hi[:, ko - 3], wo_lo[:, ko - 3])
                    nodes_at, at = slice(n * P, (n + 1) * P), slice(c * 512, (c + 1) * 512)
                    ins = passes(bank[y][:], hT_hi[:, ko, nodes_at], hT_lo[:, ko, nodes_at], hi[:, at], lo[:, at],
                                 ko == 0, ko == KO - 1)
                if kos[-1] == KO - 1:
                    ins.then_inc(o_done, 1)

            def stage2(i, do_project, attend):
                p = i - 1
                s = (i + KO) * 3

                def proj(j, part):
                    kos = ((0, 1, 2), (3, 4, 5), (6, 7))[part]
                    if do_project:
                        if part == 0 and j < 2:
                            pe.wait_ge(proj_lo_made, i * 2 + (3 * KO - 1 + j))
                        elif part == 0:
                            pe.wait_ge(proj_hi_made, s)
                        project(s + j, j, qkv_hi[j], qkv_lo[j], kos)
                    else:
                        k = j * 3 + part
                        if k < KO - 1:
                            for y in range(3):
                                out_part(y, (k,))
                        elif k == KO - 1:
                            out_part(3, range(KO - 1))

                def score(n):
                    if not attend:
                        return
                    if n == 0:
                        pe.wait_ge(proj_lo_made, p * 2 + (3 * KO + 2))
                    else:
                        pe.wait_ge(score_max, p * 6 + 2 * n)
                    at = slice(n * P, (n + 1) * P)
                    for l, r, first, last in ((q2_hi, k2_hi, True, False), (q2_hi, k2_lo, False, False),
                                              (q2_lo, k2_hi, False, True)):
                        for h in range(2):
                            rows = slice(HD * h, HD * h + HD)
                            ins = t_.matmul(bank[BANK_SCORE + h][:, 0:N], l[rows, at], r[rows], start=first, stop=last)
                            if last:
                                ins.then_inc(scored, 1)

                def turn_v():
                    if not attend:
                        return
                    pe.wait_ge(proj_hi_made, s)
                    for n in range(NT):
                        at = slice(n * P, (n + 1) * P)
                        ins = t_.transpose(bank[BANK_TURN][:, at], v2T[:, at], ident[:])
                    ins.then_inc(turned_done, 1)

                def turn(k):
                    if not attend:
                        return
                    pe.wait_ge(normed, p * 6 + k + 1)
                    if k >= 1:
                        pe.wait_ge(turn_lo, p * 7 + k)
                    for n in range(NT):
                        ins = t_.transpose(bank[BANK_TURN + (k + 1) % 2][:, n * P:(n + 1) * P],
                                           probs[:, k, n * P:(n + 1) * P], ident[:])
                    ins.then_inc(turned_done, 1)

                def pv(h):
                    if not attend:
                        return
                    pe.wait_ge(turn_lo, p * 7 + 6 + h)
                    pe.wait_ge(pv_lo, p * 2 + h + 1)
                    for m in range(NT):
                        ins = passes(bank[BANK_PV][:, 0:N], v2_hi[:, m], v2_lo[:, m], pT_hi[h][:, m], pT_lo[h][:, m],
                                     m == 0, m == NT - 1)
                    ins.then_inc(pv_done, 1)

                score(0)
                proj(0, 0)
                turn_v()
                score(1)
                proj(0, 1)
                if attend and not do_project:
                    pe.wait_ge(gsum_made, 1)
                    pe.wait_ge(pv_lo, 2 * PAIRS - 1)
                    t_.matmul(bank[BANK_PV][:, 0:2], ones[:], gsum[:], start=True, stop=True).then_inc(gsum_all, 1)
                turn(0)
                turn(1)
                score(2)
                proj(0, 2)
                turn(2)
                proj(1, 0)
                turn(3)
                proj(1, 1)
                turn(4)
                proj(1, 2)
                turn(5)
                if attend and not do_project:
                    pe.wait_ge(gsum_all, 2)
                pv(0)
                proj(2, 0)
                pv(1)
                proj(2, 1)
                proj(2, 2)

            stage2(0, True, False)
            pe.wait_ge(bits_read, 1)
            with pe.Fori(1, PAIRS) as i:
                stage2(i, True, True)
            stage2(PAIRS, False, True)
            pe.wait_ge(pv_lo, 2 * PAIRS + 1)

            def turn_tile(n):
                for half in range(2):
                    pe.wait_ge(h2_made[n], half + 1)
                    if n == 2:
                        pe.wait_ge(ln_lo, KO + half + 1)
                    for k in range(4):
                        ko = half * 4 + k
                        ins = t_.transpose(bank[H_BANKS[n][half]][:, k * P:(k + 1) * P], raw[:, n, ko * P:(ko + 1) * P],
                                           ident[:])
                    ins.then_inc(ln_turned, 1)

            def hidden(t, u, nodes_from=0, nodes_to=N, kos=range(KO)):
                pe.wait_ge(tern_made, t * 2 + 1)
                wait(pe, relu_done, t - 1)
                at = slice(nodes_from, nodes_to)
                for ko in kos:
                    for part, h in enumerate((h2_hi, h2_lo)):
                        ins = t_.matmul(bank[BANK_HID + u][:, at], tern[:, 0, u, ko * P:(ko + 1) * P], h[:, ko, at],
                                        start=(ko == 0 and part == 0), stop=(ko == KO - 1 and part == 1))
                if nodes_to == N and kos[-1] == KO - 1:
                    ins.then_inc(hid_done, 1)

            for y in range(4):
                out_part(y, (KO - 1,))
            out_part(4, range(KO))
            out_part(5, range(4))
            turn_tile(0)
            out_part(5, range(4, 6))
            turn_tile(1)
            out_part(5, range(6, KO))
            pe.wait_ge(ln_lo, KO + 4)
            hidden(0, 0, 0, 2 * P)
            hidden(1, 1, 0, 2 * P)
            turn_tile(2)
            for half in range(2):
                pe.wait_ge(ln_lo, KO + 5 + half)
                hidden(0, 0, 2 * P, N, range(half * 4, half * 4 + 4))
            hidden(1, 1, 2 * P)

            def output(t, u, first=False, last=False):
                pe.wait_ge(tern_made, t * 2 + 2)
                pe.wait_ge(act_lo_made, t + 1)
                for n in range(NT):
                    by_half = last and n == NT - 1
                    order = [(part, c) for c in range(2) for part in range(2)] if by_half else \
                            [(part, c) for part in range(2) for c in range(2)]
                    for part, c in order:
                        ins = t_.matmul(bank[BANK_Y + 2 * n + c][:], (act_hi, act_lo)[part][:, u, n * P:(n + 1) * P],
                                        tern[:, 1, u, c * 512:(c + 1) * 512],
                                        start=first and part == 0, stop=last and part == 1)
                        if last and part == 1:
                            ins.then_inc(y_done, 1)
                if not last:
                    ins.then_inc(y_step, 1)

            output(0, 0, first=True)
            with pe.Fori(1, FT // 2) as i:
                for u in range(2):
                    hidden(i * 2 + u, u)
                    if u == 0:
                        output(i * 2 - 1, 1)
                    else:
                        output(i * 2, 0)
            output(FT - 1, 1, last=True)


def kernel(x, src, dst, edge_type_5, L0_gnn_edge_type_weights, L0_gnn_wq, L0_gnn_bq, L0_gnn_wk, L0_gnn_bk,
           L0_gnn_wv, L0_gnn_bv, L0_gnn_wiq, L0_gnn_biq, L0_gnn_wik, L0_gnn_bik, L0_gnn_wiv, L0_gnn_biv,
           L0_gnn_wo, L0_gnn_bo, L0_ffn_W1, L0_ffn_b1, L0_ffn_W2, L0_ffn_b2):
    import numpy as np
    import concourse.bacc as bacc
    from concourse.bass_utils import run_bass_kernel_spmd

    def slabs(w):
        w = np.asarray(w)
        o, i = w.shape
        return w.reshape(o // P, P, i // P, P).transpose(0, 3, 2, 1).reshape(o // P, P, i)

    def turns(*ws):
        s = np.stack([slabs(w) for w in ws], axis=1)
        return s.reshape(-1, P, D)

    def columns(a):
        return np.ascontiguousarray(np.asarray(a).reshape(-1, P).T)

    w_slabs = np.concatenate([turns(L0_gnn_wq, L0_gnn_wk, L0_gnn_wv),
                              turns(L0_gnn_wiq, L0_gnn_wik, L0_gnn_wiv), np.asarray(L0_gnn_wo).T.reshape(KO, P, D)])
    biases = np.stack([columns(b) for b in (L0_gnn_bq, L0_gnn_bk, L0_gnn_bv, L0_gnn_biq, L0_gnn_bik, L0_gnn_biv)],
                      axis=1)
    ffn_slabs = np.concatenate([slabs(L0_ffn_W1), np.asarray(L0_ffn_W2).T.reshape(FT, P, D)])
    arrays = {
        "x": np.asarray(x),
        "edge_rows": np.stack([np.asarray(a).reshape(CH, P) for a in (src, dst)], axis=1),
        "edge_cols": np.stack([columns(a) for a in (src, dst, edge_type_5)], axis=1),
        "edge_w": np.asarray(L0_gnn_edge_type_weights),
        "w_slabs": w_slabs, "biases": biases, "bo": np.asarray(L0_gnn_bo), "ffn_slabs": ffn_slabs,
        "b1": columns(L0_ffn_b1), "b2": np.asarray(L0_ffn_b2),
    }
    arrays = {f"in_{k}": np.ascontiguousarray(v) for k, v in arrays.items()}
    nc = bacc.Bacc("TRN2", target_bir_lowering=False, num_devices=1)
    args = [nc.dram_tensor(k, v.shape, mybir.dt.from_np(v.dtype), kind="ExternalInput").ap() for k, v in arrays.items()]
    out = nc.dram_tensor("out", (N, D), F32, kind="ExternalOutput").ap()
    gnn_ffn_kernel(nc, *args, out)
    r = run_bass_kernel_spmd(nc, [arrays], core_ids=[0])
    return r.results[0]["out"]
```
